# Optimizing a Trainium2 kernel written in Bass

```python
import numpy as np
import jax
import jax.numpy as jnp

def _softmax(x, axis=-1):
    return jax.nn.softmax(x, axis=axis)

def _gelu(x):
    return jax.nn.gelu(x, approximate=True)

def _silu(x):
    return jax.nn.silu(x)

def _sigmoid(x):
    return jax.nn.sigmoid(x)

def _layernorm(x, axis=-1, eps=1e-05):
    m = jnp.mean(x, axis=axis, keepdims=True)
    v = jnp.var(x, axis=axis, keepdims=True)
    return (x - m) / jnp.sqrt(v + eps)

def _scatter_add(tgt, idx, src, axis=0):
    return tgt.at[idx].add(src)

def _segment_sum(src, seg, n):
    return jax.ops.segment_sum(src, seg, n)
kernel_name = 'mk_adj_resnorm_d1_adj_r2_f45fdc'

def setup_inputs(seed: int=0):
    np.random.seed(seed)
    _w = jnp.asarray

    def _rec_inputs():
        import jax
        import jax.numpy as jnp
        _gk = jax.random.key(seed)
        x = -0.0002928 + 1 * jax.random.normal(jax.random.fold_in(_gk, 1), (16, 512, 256), jnp.float32)
        _w = (1.0 + jnp.arange(512, dtype=jnp.float32)) ** (-0.5)
        _w = _w / _w.mean()
        _pij = jnp.clip(0.015625 * _w[:, None] * _w[None, :], 0.0, 1.0)
        _a = jax.random.uniform(jax.random.fold_in(_gk, 2), (16, 512, 512)) < _pij
        adj = _a.astype(jnp.int32)
        return (x, adj)
    x, adj = _rec_inputs()

    def _L0_gnn_setup():
        import jax, jax.numpy as jnp
        import numpy as np
        L = 3
        D = 256
        B, N = (8, 512)
        EPS = 1e-05

        def layernorm(x, gamma, beta):
            mu = jnp.mean(x, axis=-1, keepdims=True)
            var = jnp.var(x, axis=-1, keepdims=True)
            return (x - mu) * jax.lax.rsqrt(var + EPS) * gamma + beta
        key = jax.random.key(seed)
        ks = jax.random.split(key, 12)
        s = 1.0 / np.sqrt(D)
        node_features = jax.random.normal(ks[0], (B, N, D), dtype=jnp.float32)
        adjacency_matrix = jax.random.randint(ks[1], (B, N, N), 0, 2, dtype=jnp.int32)
        return {'node_features': node_features, 'adjacency_matrix': adjacency_matrix, 'attn_w': jax.random.normal(ks[2], (L, 2 * D), dtype=jnp.float32) * (1.0 / np.sqrt(2 * D)), 'attn_b': jax.random.normal(ks[3], (L,), dtype=jnp.float32) * 0.01, 'W1': jax.random.normal(ks[4], (L, D, 4 * D), dtype=jnp.float32) * s, 'b1': jnp.zeros((L, 4 * D), dtype=jnp.float32), 'W2': jax.random.normal(ks[5], (L, 4 * D, D), dtype=jnp.float32) * (1.0 / np.sqrt(4 * D)), 'b2': jnp.zeros((L, D), dtype=jnp.float32), 'g1': jnp.ones((L, D), dtype=jnp.float32), 'beta1': jnp.zeros((L, D), dtype=jnp.float32), 'g2': jnp.ones((L, D), dtype=jnp.float32), 'beta2': jnp.zeros((L, D), dtype=jnp.float32)}
    _L0_gnn_all = _L0_gnn_setup()
    _L0_gnn_in = {k: v for k, v in _L0_gnn_all.items() if k in ('attn_w', 'attn_b', 'W1', 'b1', 'W2', 'b2', 'g1', 'beta1', 'g2', 'beta2')}
    del _L0_gnn_all
    return {'x': x, 'adj': adj, 'L0_gnn_attn_w': _L0_gnn_in['attn_w'], 'L0_gnn_attn_b': _L0_gnn_in['attn_b'], 'L0_gnn_W1': _L0_gnn_in['W1'], 'L0_gnn_b1': _L0_gnn_in['b1'], 'L0_gnn_W2': _L0_gnn_in['W2'], 'L0_gnn_b2': _L0_gnn_in['b2'], 'L0_gnn_g1': _L0_gnn_in['g1'], 'L0_gnn_beta1': _L0_gnn_in['beta1'], 'L0_gnn_g2': _L0_gnn_in['g2'], 'L0_gnn_beta2': _L0_gnn_in['beta2']}

def reference(x, adj, L0_gnn_attn_w, L0_gnn_attn_b, L0_gnn_W1, L0_gnn_b1, L0_gnn_W2, L0_gnn_b2, L0_gnn_g1, L0_gnn_beta1, L0_gnn_g2, L0_gnn_beta2):
    import jax
    import jax.numpy as jnp

    def _L0_gnn_ref(node_features, adjacency_matrix, attn_w, attn_b, W1, b1, W2, b2, g1, beta1, g2, beta2):
        import jax, jax.numpy as jnp
        import numpy as np
        L = 3
        D = 256
        B, N = (8, 512)
        EPS = 1e-05

        def layernorm(x, gamma, beta):
            mu = jnp.mean(x, axis=-1, keepdims=True)
            var = jnp.var(x, axis=-1, keepdims=True)
            return (x - mu) * jax.lax.rsqrt(var + EPS) * gamma + beta
        n = adjacency_matrix.shape[-1]
        mask = adjacency_matrix.astype(jnp.float32) + jnp.eye(n, dtype=jnp.float32) > 0
        x = node_features
        d = x.shape[-1]
        for l in range(attn_w.shape[0]):
            si = x @ attn_w[l, :d]
            sj = x @ attn_w[l, d:]
            scores = si[:, :, None] + sj[:, None, :] + attn_b[l]
            scores = jnp.where(scores >= 0, scores, 0.2 * scores)
            scores = jnp.where(mask, scores, -jnp.inf)
            attn = jax.nn.softmax(scores, axis=-1)
            agg = jnp.einsum('bij,bjd->bid', attn, x)
            h = layernorm(x + agg, g1[l], beta1[l])
            ff = jax.nn.gelu(h @ W1[l] + b1[l], approximate=False) @ W2[l] + b2[l]
            x = layernorm(h + ff, g2[l], beta2[l])
        return x
    x = _layernorm(x + _L0_gnn_ref(x, adj, L0_gnn_attn_w, L0_gnn_attn_b, L0_gnn_W1, L0_gnn_b1, L0_gnn_W2, L0_gnn_b2, L0_gnn_g1, L0_gnn_beta1, L0_gnn_g2, L0_gnn_beta2), axis=-1)
    return x

_drawn_inputs = setup_inputs


def setup_inputs(seed=0):
    import zlib

    import numpy as np

    out = dict(_drawn_inputs(seed))
    spreads = {'L0_gnn_b1': (0.0, 0.1),
     'L0_gnn_b2': (0.0, 0.1),
     'L0_gnn_g1': (1.0, 0.2),
     'L0_gnn_beta1': (0.0, 0.1),
     'L0_gnn_g2': (1.0, 0.2),
     'L0_gnn_beta2': (0.0, 0.1)}
    factors = {'L0_gnn_attn_b': 64.0}
    for name, (base, spread) in spreads.items():
        noise = np.random.default_rng([zlib.crc32(name.encode()), seed]).standard_normal(out[name].shape)
        drawn = base * np.exp(spread * noise) if base else spread * noise
        out[name] = jnp.asarray(drawn.astype(out[name].dtype))
    for name, factor in factors.items():
        out[name] = (out[name] * factor).astype(out[name].dtype)
    return out
```

```python
from contextlib import ExitStack

import concourse.bass as bass
from concourse import mybir

ALU = mybir.AluOpType
ACT = mybir.ActivationFunctionType
F32 = mybir.dt.float32
F32R = mybir.dt.float32r
BF16 = mybir.dt.bfloat16
I32 = mybir.dt.int32

P = 128
EPS = 1e-5
SLOPE = 0.2
BIG = 1e30
LOWEST = -3e38

UNIT = 16
F1_BANKS = 3
G_RING = 4
POOL_LO = (6, 7)


def steps(done, of):
    assert UNIT % of == 0
    return done * (UNIT // of)


class Unit:

    def __init__(self, layer, graph16, graphs):
        self.layer, self.graph16, self.graphs = layer, graph16, graphs
        self.at = graph16 + layer * graphs * UNIT

    def has_before(self, n=1):
        return not isinstance(self.at, int) or self.at >= n * UNIT

    def first_of_layer(self):
        return isinstance(self.graph16, int) and self.graph16 == 0

    def is_first(self):
        return isinstance(self.at, int) and self.at == 0


def gnn_program(nc, x, adj, attn_w, attn_b, w1, b1, w2, b2, g1, beta1, g2, beta2, out):
    B, N, D = x.shape
    L, _, F = w1.shape
    NT = N // P
    DT = D // P
    FT = F // P
    NP = NT // 2
    assert NT == 4 and 2 * D == 512 and N == 512 and UNIT % FT == 0

    x_mid = nc.dram_tensor("x_mid", [(L - 1) * B * P, NT * D], F32)
    x_rows = x.rearrange("b n d -> (b n) d")
    out_rows = out.rearrange("b n d -> (b n) d")
    adj_rows = adj.rearrange("b i j -> (b i) j")

    def node_rows(flat, first):
        return flat[bass.ds(first, N), :].rearrange("(t p) d -> p t d", p=P)

    with ExitStack() as ctx:
        def sb(name, shape, dt=F32):
            return ctx.enter_context(nc.sbuf_tensor(name, shape, dt))

        def psum(name):
            return ctx.enter_context(nc.psum_tensor(name, [P, 512], F32))

        def sem(name):
            return ctx.enter_context(nc.semaphore(name))

        ident = sb("ident", [P, P])
        eye_int = sb("eye_int", [P, P], I32)
        eps_t = sb("eps_t", [P, NT])
        neg_half = sb("neg_half", [P, NT])
        neg_one = sb("neg_one", [P, NT])
        attn_w_bc = sb("attn_w_bc", [P, L, 2, D])
        attn_b_bc = sb("attn_b_bc", [P, L])
        g1_bc = sb("g1_bc", [P, L, D])
        beta1_bc = sb("beta1_bc", [P, L, D])
        b2_bc = sb("b2_bc", [P, L, D])
        g2_bc = sb("g2_bc", [P, L, D])
        beta2_bc = sb("beta2_bc", [P, L, D])
        b1_col = sb("b1_col", [P, L, FT])
        w_stage = sb("w_stage", [P, DT * F])
        w1_hi = sb("w1_hi", [P, DT, F], F32R)
        w1_lo = sb("w1_lo", [P, DT, F], F32R)
        w2_hi = sb("w2_hi", [P, FT, D], F32R)
        w2_lo = sb("w2_lo", [P, FT, D], F32R)
        adj_t = sb("adj_t", [P, NT, N], I32)
        no_edge = sb("no_edge", [P, NT, N], BF16)
        x_t = sb("x_t", [P, NT, D])
        x_hi = sb("x_hi", [P, NT, D], F32R)
        x_lo = sb("x_lo", [P, NT, D], F32R)
        dot_junk = sb("dot_junk", [P, 4, D], BF16)
        s_i = sb("s_i", [P, NT])
        s_j = sb("s_j", [P, NT])
        row_max = sb("row_max", [P, NT])
        top = sb("top", [P, NT])
        top_leaky = sb("top_leaky", [P, NT])
        shift_pos = sb("shift_pos", [P, NT])
        shift_neg = sb("shift_neg", [P, NT])
        score = sb("score", [P, NT, N])
        prob = sb("prob", [P, NT, N])
        denom = sb("denom", [P, NT])
        x_res = sb("x_res", [P, NT, D])
        recip = sb("recip", [P, NT])
        pt_hi = sb("pt_hi", [P, NT, N], F32R)
        pt_lo = sb("pt_lo", [P, NT, N], F32R)
        y1 = sb("y1", [P, NT, D])
        stats1 = sb("stats1", [P, NT, 6])
        mv1 = sb("mv1", [P, NT, 2])
        var1 = sb("var1", [P, NT])
        rstd1 = sb("rstd1", [P, NT])
        h = sb("h", [P, NT, D])
        ht_hi = sb("ht_hi", [P, DT, N], F32R)
        ht_lo = sb("ht_lo", [P, DT, N], F32R)
        h_b2 = sb("h_b2", [P, NT, D])
        hid = sb("hid", [P, G_RING, N])
        hid_hi = sb("hid_hi", [P, FT, N], F32R)
        hid_lo = sb("hid_lo", [P, FT, N], F32R)
        y2 = sb("y2", [P, NT, D])
        stats2 = sb("stats2", [P, NT, 6])
        mv2 = sb("mv2", [P, NT, 2])
        var2 = sb("var2", [P, NT])
        rstd2 = sb("rstd2", [P, NT])
        mr2 = sb("mr2", [P, NT])
        nmr2 = sb("nmr2", [P, NT])
        x_new = sb("x_new", [P, NT, D])
        x_first = sb("x_first", [P, NT, D])
        stats3 = sb("stats3", [P, NT, 6])
        mv3 = sb("mv3", [P, NT, 2])
        var3 = sb("var3", [P, NT])
        rstd3 = sb("rstd3", [P, NT])
        mr3 = sb("mr3", [P, NT])
        nmr3 = sb("nmr3", [P, NT])

        ps_hid = [psum(f"ps_hid{i}") for i in range(F1_BANKS)]
        ps_turn = [psum(f"ps_turn{i}") for i in range(2)]
        ps_acc = [psum(f"ps_acc{i}") for i in range(NP)]
        ps_sj = psum("ps_sj")

        params_in = sem("params_in")
        consts_set = sem("consts_set")
        ident_set = sem("ident_set")
        w_in = sem("w_in")
        w_hi_set = sem("w_hi_set")
        w_lo_set = sem("w_lo_set")
        adj_in = sem("adj_in")
        x_in = sem("x_in")
        x_res_in = sem("x_res_in")
        x_first_in = sem("x_first_in")
        stored = sem("stored")
        diag_set = sem("diag_set")
        masked = sem("masked")
        dotted = sem("dotted")
        spread = sem("spread")
        scored = sem("scored")
        shifted = sem("shifted")
        exped = sem("exped")
        prob_set = sem("prob_set")
        x_hi_set = sem("x_hi_set")
        x_lo_set = sem("x_lo_set")
        turned = sem("turned")
        pt_hi_set = sem("pt_hi_set")
        pt_lo_set = sem("pt_lo_set")
        recip_set = sem("recip_set")
        agg_done = sem("agg_done")
        y1_set = sem("y1_set")
        moments1 = sem("moments1")
        rstd1_set = sem("rstd1_set")
        centered1 = sem("centered1")
        h_set = sem("h_set")
        h_turned = sem("h_turned")
        ht_hi_set = sem("ht_hi_set")
        ht_lo_set = sem("ht_lo_set")
        h_b2_set = sem("h_b2_set")
        hid_done = sem("hid_done")
        hid_set = sem("hid_set")
        hid_hi_set = sem("hid_hi_set")
        hid_lo_vec = sem("hid_lo_vec")
        hid_lo_pool = sem("hid_lo_pool")
        ff_done = sem("ff_done")
        y2_set = sem("y2_set")
        moments2 = sem("moments2")
        rstd2_set = sem("rstd2_set")
        normed2 = sem("normed2")
        scaled2 = sem("scaled2")
        x_new_set = sem("x_new_set")
        y3_set = sem("y3_set")
        moments3 = sem("moments3")
        rstd3_set = sem("rstd3_set")
        normed3 = sem("normed3")

        VEC_LO = [k for k in range(FT) if k not in POOL_LO]
        N_PARAMS = 8

        def last(u):
            return u.layer == L - 1

        def at_last(u):
            return u.graph16

        def slots(eng, slot):
            def unit(i):
                return Unit(i // B, i % B * UNIT, B) if 0 <= i < L * B else None

            def peeled(i):
                slot(unit(i - 1), unit(i), unit(i + 1), unit(i + 2))

            peeled(-2)
            peeled(-1)
            for layer in range(L):
                first = 2 if layer == 0 else 1
                for graph in range(first):
                    peeled(layer * B + graph)
                with eng.Fori(first, B - 2) as graph:
                    slot(*(Unit(layer, (graph + k) * UNIT, B) for k in (-1, 0, 1, 2)))
                peeled(layer * B + B - 2)
                peeled(layer * B + B - 1)
            peeled(L * B)

        block = ctx.enter_context(nc.Block())

        @block.sync
        def _(sp):
            def load_weights(n):
                if n:
                    sp.wait_ge(w_hi_set, n)
                    sp.wait_ge(w_lo_set, n)
                layer, second = divmod(n, 2)
                w, k = (w2, FT) if second else (w1, DT)
                sp.dma_start(w_stage[:, :].rearrange("p (k f) -> p k f", k=k),
                             w[layer].rearrange("(k p) f -> p k f", p=P)).then_inc(w_in, 16)

            def known(value):
                return value if isinstance(value, int) else sp.snap(sp.to_reg(value))

            def source_of_x(u):
                if u.layer == 0:
                    return node_rows(x_rows, known(u.graph16 * (N // UNIT))), None
                here = known(u.graph16 * (P // UNIT) + (u.layer - 1) * B * P)
                return x_mid[bass.ds(here, P), :], known(u.at + UNIT - B * UNIT)

            def load_x(tile, source, layer_before, signal):
                if layer_before is not None:
                    sp.wait_ge(stored, layer_before)
                    sp.dma_start(tile[:, :, :].rearrange("p t d -> p (t d)"), source).then_inc(signal, 16)
                else:
                    sp.dma_start(tile[:, :, :], source).then_inc(signal, 16)

            def load_prepare(u):
                source, layer_before = source_of_x(u)
                adj_source = node_rows(adj_rows, known(u.graph16 * (N // UNIT)))
                at = known(u.at)
                if u.has_before():
                    sp.wait_ge(dotted, at)
                    sp.wait_ge(x_lo_set, at)
                load_x(x_t, source, layer_before, x_in)
                if u.has_before():
                    sp.wait_ge(masked, at)
                sp.dma_start(adj_t[:, :, :], adj_source).then_inc(adj_in, 16)

            def load_residual(u):
                source, layer_before = source_of_x(u)
                at = known(u.at)
                if u.has_before():
                    sp.wait_ge(y1_set, at)
                load_x(x_res, source, layer_before, x_res_in)

            def load_first(u):
                source = node_rows(x_rows, known(u.graph16 * (N // UNIT)))
                at = known(at_last(u))
                if not u.first_of_layer():
                    sp.wait_ge(y3_set, at)
                sp.dma_start(x_first[:, :, :], source).then_inc(x_first_in, 16)

            def store(u):
                at = known(u.at)
                if last(u):
                    ready, full = normed3, known(at_last(u) + UNIT)
                    target = node_rows(out_rows, known(u.graph16 * (N // UNIT)))
                    tile = x_new[:, :, :]
                else:
                    ready, full = x_new_set, known(u.at + UNIT)
                    target = x_mid[bass.ds(known(u.graph16 * (P // UNIT) + u.layer * B * P), P), :]
                    tile = x_new[:, :, :].rearrange("p t d -> p (t d)")
                if u.has_before():
                    sp.wait_ge(stored, at)
                sp.wait_ge(ready, full)
                sp.dma_start(target, tile).then_inc(stored, 16)

            load_prepare(Unit(0, 0, B))
            sp.dma_start(attn_w_bc[:, :, :, :].rearrange("p l s d -> p (l s d)"),
                         attn_w.rearrange("l s -> (l s)").partition_broadcast(P)).then_inc(params_in, 16)
            sp.dma_start(attn_b_bc[:, :], attn_b.partition_broadcast(P)).then_inc(params_in, 16)
            load_weights(0)
            for tile, param in ((g1_bc, g1), (beta1_bc, beta1), (b2_bc, b2), (g2_bc, g2), (beta2_bc, beta2)):
                sp.dma_start(tile[:, :, :].rearrange("p l d -> p (l d)"),
                             param.rearrange("l d -> (l d)").partition_broadcast(P)).then_inc(params_in, 16)
            with nc.allow_non_contiguous_dma(reason="b1 by partition, once"):
                sp.dma_start(b1_col[:, :, :], b1.rearrange("l (k p) -> p l k", p=P)).then_inc(params_in, 16)

            def slot(prev, u, v, w):
                if w and not w.is_first():
                    load_prepare(w)
                if v and v.is_first():
                    load_weights(1)
                if v:
                    load_residual(v)
                if prev and last(prev):
                    load_first(prev)
                if prev:
                    store(prev)
                if u and u.first_of_layer() and u.layer > 0:
                    load_weights(2 * u.layer + 1)
                if u and u.first_of_layer() and u.layer + 1 < L:
                    load_weights(2 * u.layer + 2)

            slots(sp, slot)
            sp.wait_ge(stored, L * B * UNIT)

        @block.gpsimd
        def _(pool):
            tt = nc.gpsimd.tensor_tensor

            def weight_lo(n):
                hi, lo = (w2_hi, w2_lo) if n % 2 else (w1_hi, w1_lo)
                k = FT if n % 2 else DT
                pool.wait_ge(w_hi_set, n + 1)
                tt(lo[:, :, :], w_stage[:, :].rearrange("p (k f) -> p k f", k=k), hi[:, :, :],
                   ALU.subtract).then_inc(w_lo_set, 1)

            def self_loops(u):
                for t in range(NT):
                    if t == 0:
                        pool.wait_ge(adj_in, u.at + UNIT)
                    blk = adj_t[:, t, t * P:(t + 1) * P]
                    tt(blk, blk, eye_int[:, :], ALU.add).then_inc(diag_set, steps(1, NT))

            def split_x(u):
                pool.wait_ge(x_hi_set, u.at + UNIT)
                tt(x_lo[:, :, :], x_t[:, :, :], x_hi[:, :, :], ALU.subtract).then_inc(x_lo_set, UNIT)

            def rstd_of(u_at, pair, moments, mv, var, rstd, signal, of):
                s = slice(2 * pair, 2 * pair + 2)
                pool.wait_ge(moments, u_at + steps(4 * pair + 4, 8))
                tt(var[:, s], mv[:, s, 1], eps_t[:, s], ALU.add).then_inc(signal, steps(1, of))
                pool.wait_ge(signal, u_at + steps((pair * of) // 2 + 1, of))
                tt(rstd[:, s], var[:, s], neg_half[:, s], ALU.pow).then_inc(signal, steps(1, of))

            def offset_of(u_at, pair, mv, rstd, mr, nmr, signal):
                s = slice(2 * pair, 2 * pair + 2)
                pool.wait_ge(signal, u_at + steps(4 * pair + 2, 8))
                tt(mr[:, s], mv[:, s, 0], rstd[:, s], ALU.mult).then_inc(signal, steps(1, 8))
                pool.wait_ge(signal, u_at + steps(4 * pair + 3, 8))
                tt(nmr[:, s], mr[:, s], neg_one[:, s], ALU.mult).then_inc(signal, steps(1, 8))

            def add_b2(u):
                if u.has_before():
                    pool.wait_ge(y2_set, u.at)
                for t in range(NT):
                    pool.wait_ge(h_set, u.at + steps(t + 1, NT))
                    tt(h_b2[:, t, :], h[:, t, :], b2_bc[:, u.layer, :], ALU.add).then_inc(h_b2_set, steps(1, NT))

            def affine2(u):
                for t in range(NT):
                    pool.wait_ge(normed2, u.at + steps(t + 1, NT))
                    tt(x_new[:, t, :], x_new[:, t, :], g2_bc[:, u.layer, :], ALU.mult)\
                        .then_inc(scaled2, steps(1, NT))
                for t in range(NT):
                    pool.wait_ge(scaled2, u.at + steps(t + 1, NT))
                    tt(x_new[:, t, :], x_new[:, t, :], beta2_bc[:, u.layer, :], ALU.add)\
                        .then_inc(x_new_set, steps(1, NT))

            def hidden_lo(u, n):
                k = POOL_LO[n]
                if n == 0 and u.has_before():
                    pool.wait_ge(ff_done, u.at)
                pool.wait_ge(hid_hi_set, u.at + steps(k + 1, FT))
                tt(hid_lo[:, k, :], hid[:, k % G_RING, :], hid_hi[:, k, :], ALU.subtract)\
                    .then_inc(hid_lo_pool, steps(1, len(POOL_LO)))

            nc.gpsimd.memset(ident[:, :], 0.0).then_inc(ident_set, 1)
            nc.gpsimd.memset(eye_int[:, :], 0).then_inc(ident_set, 1)
            nc.gpsimd.memset(eps_t[:, :], EPS).then_inc(consts_set, 1)
            nc.gpsimd.memset(neg_half[:, :], -0.5).then_inc(consts_set, 1)
            nc.gpsimd.memset(neg_one[:, :], -1.0).then_inc(consts_set, 1)
            pool.wait_ge(ident_set, 2)
            nc.gpsimd.affine_select(out=ident[:, :], in_=ident[:, :], compare_op=ALU.not_equal, fill=1.0,
                                    base=0, pattern=[[-1, P]], channel_multiplier=1).then_inc(ident_set, 1)
            pool.wait_ge(ident_set, 3)
            nc.gpsimd.tensor_copy(eye_int[:, :], ident[:, :]).then_inc(ident_set, 1)
            pool.wait_ge(ident_set, 4)
            pool.wait_ge(consts_set, 3)
            pool.wait_ge(params_in, 16 * N_PARAMS)

            def slot(prev, u, v, w):
                if prev:
                    rstd_of(prev.at, 0, moments2, mv2, var2, rstd2, rstd2_set, 8)
                    offset_of(prev.at, 0, mv2, rstd2, mr2, nmr2, rstd2_set)
                if w:
                    self_loops(w)
                if prev:
                    rstd_of(prev.at, 1, moments2, mv2, var2, rstd2, rstd2_set, 8)
                    offset_of(prev.at, 1, mv2, rstd2, mr2, nmr2, rstd2_set)
                if u:
                    add_b2(u)
                if prev:
                    affine2(prev)
                if u and u.first_of_layer() and u.layer > 0:
                    weight_lo(2 * u.layer + 1)
                if u:
                    for n in range(len(POOL_LO)):
                        hidden_lo(u, n)
                if prev and last(prev):
                    for pair in range(NP):
                        rstd_of(at_last(prev), pair, moments3, mv3, var3, rstd3, rstd3_set, 8)
                        offset_of(at_last(prev), pair, mv3, rstd3, mr3, nmr3, rstd3_set)
                if v and v.is_first():
                    weight_lo(0)
                if v:
                    for pair in range(NP):
                        rstd_of(v.at, pair, moments1, mv1, var1, rstd1, rstd1_set, 4)
                if v and v.is_first():
                    weight_lo(1)
                if w:
                    split_x(w)
                if v and v.first_of_layer() and v.layer > 0:
                    weight_lo(2 * v.layer)

            slots(pool, slot)

        @block.scalar
        def _(act):
            def weight_hi(n):
                hi, k = (w2_hi, FT) if n % 2 else (w1_hi, DT)
                act.wait_ge(w_in, 16 * (n + 1))
                if n > 1:
                    act.wait_ge(ff_done if n % 2 else hid_done, n // 2 * B * UNIT)
                nc.scalar.activation(hi[:, :, :], w_stage[:, :].rearrange("p (k f) -> p k f", k=k), ACT.Copy)\
                    .then_inc(w_hi_set, 1)

            def mask(u):
                act.wait_ge(diag_set, u.at + UNIT)
                if u.has_before():
                    act.wait_ge(scored, u.at)
                nc.scalar.activation(no_edge[:, :, :], adj_t[:, :, :], ACT.Relu, bias=BIG, scale=-BIG)\
                    .then_inc(masked, UNIT)

            def exps(u, t):
                if t == 0:
                    act.wait_ge(shifted, u.at + UNIT)
                    if u.has_before():
                        act.wait_ge(turned, u.at)
                nc.scalar.activation(prob[:, t, :], score[:, t, :], ACT.Exp, bias=shift_pos[:, t:t + 1])\
                    .then_inc(exped, steps(1, 2 * NT))
                act.wait_ge(exped, u.at + steps(2 * t + 1, 2 * NT))
                nc.scalar.activation(score[:, t, :], score[:, t, :], ACT.Exp, bias=shift_neg[:, t:t + 1],
                                     scale=SLOPE).then_inc(exped, steps(1, 2 * NT))

            def split_x(u):
                act.wait_ge(x_in, u.at + UNIT)
                if u.has_before():
                    act.wait_ge(agg_done, u.at)
                nc.scalar.activation(x_hi[:, :, :], x_t[:, :, :], ACT.Copy).then_inc(x_hi_set, UNIT)

            def prob_hi(u, jt):
                if jt == 0 and u.has_before():
                    act.wait_ge(agg_done, u.at)
                act.wait_ge(turned, u.at + steps(jt + 1, NT))
                nc.scalar.activation(pt_hi[:, jt, :], ps_turn[jt % 2][:, :], ACT.Copy)\
                    .then_inc(pt_hi_set, steps(1, NT))

            def h_hi(u, pair):
                if pair == 0 and u.has_before():
                    act.wait_ge(hid_done, u.at)
                act.wait_ge(h_turned, u.at + steps(pair + 1, NP))
                nc.scalar.activation(ht_hi[:, :, pair * 2 * P:(pair + 1) * 2 * P],
                                     ps_turn[pair][:, :].rearrange("p (k n) -> p k n", k=DT), ACT.Copy)\
                    .then_inc(ht_hi_set, steps(1, NP))

            def gelu(u, k):
                if k >= G_RING or u.has_before():
                    free = k - G_RING
                    back = u.at if free >= 0 else u.at - UNIT
                    free %= FT
                    if free in POOL_LO:
                        act.wait_ge(hid_lo_pool, back + steps(POOL_LO.index(free) + 1, len(POOL_LO)))
                    else:
                        act.wait_ge(hid_lo_vec, back + steps(free + 1, FT))
                act.wait_ge(hid_done, u.at + steps(k + 1, FT))
                nc.scalar.activation(hid[:, k % G_RING, :], ps_hid[k % F1_BANKS][:, :], ACT.Gelu,
                                     bias=b1_col[:, u.layer, k:k + 1]).then_inc(hid_set, steps(1, FT))

            def hidden_hi(u, k):
                if k == 0 and u.has_before():
                    act.wait_ge(ff_done, u.at)
                act.wait_ge(hid_set, u.at + steps(k + 1, FT))
                nc.scalar.activation(hid_hi[:, k, :], hid[:, k % G_RING, :], ACT.Copy)\
                    .then_inc(hid_hi_set, steps(1, FT))

            def normalize2(u, pair):
                act.wait_ge(rstd2_set, u.at + steps(4 * pair + 4, 8))
                if pair == 0 and u.has_before():
                    act.wait_ge(stored, u.at)
                for t in (2 * pair, 2 * pair + 1):
                    nc.scalar.activation(x_new[:, t, :], y2[:, t, :], ACT.Identity, bias=nmr2[:, t:t + 1],
                                         scale=rstd2[:, t:t + 1]).then_inc(normed2, steps(1, NT))

            def normalize3(u, pair):
                act.wait_ge(rstd3_set, at_last(u) + steps(4 * pair + 4, 8))
                for t in (2 * pair, 2 * pair + 1):
                    nc.scalar.activation(x_new[:, t, :], x_new[:, t, :], ACT.Identity, bias=nmr3[:, t:t + 1],
                                         scale=rstd3[:, t:t + 1]).then_inc(normed3, steps(1, NT))

            act.wait_ge(params_in, 16 * N_PARAMS)

            def slot(prev, u, v, w):
                for k in range(FT):
                    if u:
                        gelu(u, k)
                        if k > 0:
                            hidden_hi(u, k - 1)
                    if w and k == 1:
                        mask(w)
                    if prev and k in (3, 4):
                        normalize2(prev, k - 3)
                    if v and k == 5:
                        prob_hi(v, 0)
                        prob_hi(v, 1)
                    if v and k == 6:
                        prob_hi(v, 2)
                        prob_hi(v, 3)
                if u:
                    hidden_hi(u, FT - 1)
                if u and u.first_of_layer() and u.layer > 0:
                    weight_hi(2 * u.layer + 1)
                if prev and last(prev):
                    for pair in range(NP):
                        normalize3(prev, pair)
                if v and v.is_first():
                    weight_hi(0)
                if w:
                    for t in range(NT):
                        exps(w, t)
                    split_x(w)
                if v:
                    if v.is_first():
                        weight_hi(1)
                    if v.first_of_layer() and v.layer > 0:
                        weight_hi(2 * v.layer)
                    for pair in range(NP):
                        h_hi(v, pair)

            slots(act, slot)

        @block.tensor
        def _(pe):
            def hidden(u, k):
                if k == 0:
                    pe.wait_ge(ht_lo_set, u.at + UNIT)
                    if u.first_of_layer():
                        pe.wait_ge(w_lo_set, 2 * u.layer + 1)
                if k >= F1_BANKS or u.has_before():
                    free = k - F1_BANKS
                    if free < 0:
                        free = max(j for j in range(FT) if j % F1_BANKS == k) - FT
                    pe.wait_ge(hid_set, u.at + steps(free + 1, FT))
                cols = slice(k * P, (k + 1) * P)
                terms = [(w, ht, d) for d in range(DT) for w, ht in ((w1_hi, ht_hi), (w1_hi, ht_lo), (w1_lo, ht_hi))]
                for n, (w, ht, d) in enumerate(terms):
                    mm = nc.tensor.matmul(ps_hid[k % F1_BANKS][:, :], w[:, d, cols], ht[:, d, :],
                                          start=(n == 0), stop=(n == len(terms) - 1))
                mm.then_inc(hid_done, steps(1, FT))

            def turn_prob(u, jt):
                if jt == 0:
                    pe.wait_ge(prob_set, u.at + UNIT)
                if jt >= 2:
                    pe.wait_ge(pt_lo_set, u.at + steps(jt - 1, NT))
                elif u.has_before():
                    pe.wait_ge(ht_lo_set, u.at - UNIT + steps(jt + 1, NP))
                for it in range(NT):
                    mm = nc.tensor.transpose(ps_turn[jt % 2][:, it * P:(it + 1) * P],
                                             prob[:, it, jt * P:(jt + 1) * P], ident[:, :])
                mm.then_inc(turned, steps(1, NT))

            def spread_sj(u):
                pe.wait_ge(dotted, u.at + UNIT)
                if u.has_before():
                    pe.wait_ge(scored, u.at)
                for t in range(NT):
                    mm = nc.tensor.matmul(ps_sj[:, t * P:(t + 1) * P], s_j[:, t:t + 1].to_broadcast([P, P]),
                                          ident[:, :], start=True, stop=True)
                mm.then_inc(spread, UNIT)

            def aggregate(u, pair):
                if pair == 0:
                    pe.wait_ge(pt_lo_set, u.at + UNIT)
                    pe.wait_ge(x_lo_set, u.at + UNIT)
                if u.has_before(2):
                    pe.wait_ge(y2_set, u.at - 2 * UNIT + steps(2 * pair + 2, NT))
                for half in range(2):
                    t = 2 * pair + half
                    cols = slice(t * P, (t + 1) * P)
                    terms = [(p, xs, jt) for jt in range(NT)
                             for p, xs in ((pt_hi, x_hi), (pt_hi, x_lo), (pt_lo, x_hi))]
                    for n, (p, xs, jt) in enumerate(terms):
                        mm = nc.tensor.matmul(ps_acc[pair][:, half * D:(half + 1) * D], p[:, jt, cols],
                                              xs[:, jt, :], start=(n == 0), stop=(n == len(terms) - 1))
                mm.then_inc(agg_done, steps(1, NP))

            def feed(u, t, next_unit):
                pair, half = divmod(t, 2)
                if t == 0:
                    pe.wait_ge(hid_lo_vec, u.at + UNIT)
                    pe.wait_ge(hid_lo_pool, u.at + UNIT)
                    if u.first_of_layer():
                        pe.wait_ge(w_lo_set, 2 * u.layer + 2)
                if half == 0 and next_unit:
                    pe.wait_ge(y1_set, next_unit.at + steps(2 * pair + 2, NT))
                cols = slice(t * P, (t + 1) * P)
                terms = [(g, w, k) for k in range(FT) for g, w in ((hid_hi, w2_hi), (hid_hi, w2_lo), (hid_lo, w2_hi))]
                for n, (g, w, k) in enumerate(terms):
                    mm = nc.tensor.matmul(ps_acc[pair][:, half * D:(half + 1) * D], g[:, k, cols], w[:, k, :],
                                          start=(n == 0), stop=(n == len(terms) - 1))
                if half:
                    mm.then_inc(ff_done, steps(1, NP))

            def turn_h(u, pair):
                pe.wait_ge(h_set, u.at + steps(2 * pair + 2, NT))
                pe.wait_ge(pt_lo_set, u.at + steps(pair + 3, NT))
                for d in range(DT):
                    for half in range(2):
                        mm = nc.tensor.transpose(ps_turn[pair][:, (2 * d + half) * P:(2 * d + half + 1) * P],
                                                 h[:, 2 * pair + half, d * P:(d + 1) * P], ident[:, :])
                mm.then_inc(h_turned, steps(1, NP))

            pe.wait_ge(ident_set, 3)

            def slot(prev, u, v, w):
                for k in range(FT):
                    if u:
                        hidden(u, k)
                    if v and k == 5:
                        turn_prob(v, 0)
                        turn_prob(v, 1)
                    if v and k == 6:
                        turn_prob(v, 2)
                        turn_prob(v, 3)
                if w:
                    spread_sj(w)
                if v:
                    aggregate(v, 0)
                    aggregate(v, 1)
                if u:
                    feed(u, 0, v)
                    feed(u, 1, v)
                if v:
                    turn_h(v, 0)
                if u:
                    feed(u, 2, v)
                if v:
                    turn_h(v, 1)
                if u:
                    feed(u, 3, v)

            slots(pe, slot)

        @block.vector
        def _(dve):
            v_ = nc.vector

            def dots(u, t):
                if t == 0:
                    dve.wait_ge(x_in, u.at + UNIT)
                    if u.has_before():
                        dve.wait_ge(spread, u.at)
                        dve.wait_ge(prob_set, u.at)
                elif t >= 2:
                    dve.wait_ge(dotted, u.at + steps(2 * t - 2, 2 * NT))
                v_.tensor_tensor_reduce(dot_junk[:, 2 * t % 4, :], x_t[:, t, :], attn_w_bc[:, u.layer, 0, :],
                                        1.0, attn_b_bc[:, u.layer:u.layer + 1], ALU.mult, ALU.add,
                                        s_i[:, t:t + 1]).then_inc(dotted, steps(1, 2 * NT))
                v_.tensor_tensor_reduce(dot_junk[:, (2 * t + 1) % 4, :], x_t[:, t, :], attn_w_bc[:, u.layer, 1, :],
                                        1.0, 0.0, ALU.mult, ALU.add,
                                        s_j[:, t:t + 1]).then_inc(dotted, steps(1, 2 * NT))

            def scores(u, t):
                if t == 0:
                    dve.wait_ge(spread, u.at + UNIT)
                    dve.wait_ge(masked, u.at + UNIT)
                v_.tensor_tensor_reduce(score[:, t, :], ps_sj[:, :], no_edge[:, t, :], 1.0, LOWEST,
                                        ALU.subtract, ALU.max, row_max[:, t:t + 1])\
                    .then_inc(scored, steps(1, NT))

            def shifts(u):
                dve.wait_ge(scored, u.at + UNIT)
                v_.tensor_tensor(top[:, :], row_max[:, :], s_i[:, :], ALU.add).then_inc(shifted, steps(1, 4))
                dve.wait_ge(shifted, u.at + steps(1, 4))
                v_.scalar_tensor_tensor(out=top_leaky[:, :], in0=top[:, :], scalar=SLOPE, in1=top[:, :],
                                        op0=ALU.mult, op1=ALU.max).then_inc(shifted, steps(1, 4))
                dve.wait_ge(shifted, u.at + steps(2, 4))
                v_.tensor_tensor(shift_pos[:, :], s_i[:, :], top_leaky[:, :], ALU.subtract)\
                    .then_inc(shifted, steps(1, 4))
                v_.scalar_tensor_tensor(out=shift_neg[:, :], in0=s_i[:, :], scalar=SLOPE, in1=top_leaky[:, :],
                                        op0=ALU.mult, op1=ALU.subtract).then_inc(shifted, steps(1, 4))

            def probs(u, t):
                dve.wait_ge(exped, u.at + steps(2 * t + 2, 2 * NT))
                v_.scalar_tensor_tensor(out=prob[:, t, :], in0=prob[:, t, :], scalar=1.0, in1=score[:, t, :],
                                        op0=ALU.mult, op1=ALU.max, accum_out=denom[:, t:t + 1])\
                    .then_inc(prob_set, steps(1, NT))

            def prob_lo(u, jt):
                if jt == 0 and u.has_before():
                    dve.wait_ge(agg_done, u.at)
                dve.wait_ge(pt_hi_set, u.at + steps(jt + 1, NT))
                v_.tensor_tensor(pt_lo[:, jt, :], ps_turn[jt % 2][:, :], pt_hi[:, jt, :], ALU.subtract)\
                    .then_inc(pt_lo_set, steps(1, NT))

            def reciprocals(u):
                dve.wait_ge(prob_set, u.at + UNIT)
                v_.reciprocal(recip[:, :], denom[:, :]).then_inc(recip_set, UNIT)

            def residual1(u, pair):
                dve.wait_ge(agg_done, u.at + steps(pair + 1, NP))
                if pair == 0:
                    dve.wait_ge(recip_set, u.at + UNIT)
                    dve.wait_ge(x_res_in, u.at + UNIT)
                for half in range(2):
                    t = 2 * pair + half
                    v_.scalar_tensor_tensor(out=y1[:, t, :], in0=ps_acc[pair][:, half * D:(half + 1) * D],
                                            scalar=recip[:, t:t + 1], in1=x_res[:, t, :],
                                            op0=ALU.mult, op1=ALU.add).then_inc(y1_set, steps(1, NT))

            def moments(at, pair, ready, y, stats, mv, signal):
                for half in range(2):
                    t = 2 * pair + half
                    dve.wait_ge(ready, at + steps(t + 1, NT))
                    v_.bn_stats(stats[:, t, :], y[:, t, :]).then_inc(signal, steps(1, 8))
                for half in range(2):
                    t = 2 * pair + half
                    dve.wait_ge(signal, at + steps(4 * pair + 1 + half, 8))
                    v_.bn_aggr(mv[:, t, :], stats[:, t, :]).then_inc(signal, steps(1, 8))

            def affine1(u, pair):
                dve.wait_ge(rstd1_set, u.at + steps(2 * pair + 2, 4))
                if pair == 0 and u.has_before():
                    dve.wait_ge(h_turned, u.at)
                    dve.wait_ge(h_b2_set, u.at)
                for t in (2 * pair, 2 * pair + 1):
                    v_.scalar_tensor_tensor(out=h[:, t, :], in0=y1[:, t, :], scalar=mv1[:, t, 0:1],
                                            in1=g1_bc[:, u.layer, :], op0=ALU.subtract, op1=ALU.mult)\
                        .then_inc(centered1, steps(1, NT))
                for t in (2 * pair, 2 * pair + 1):
                    dve.wait_ge(centered1, u.at + steps(t + 1, NT))
                    v_.scalar_tensor_tensor(out=h[:, t, :], in0=h[:, t, :], scalar=rstd1[:, t:t + 1],
                                            in1=beta1_bc[:, u.layer, :], op0=ALU.mult, op1=ALU.add)\
                        .then_inc(h_set, steps(1, NT))

            def h_lo(u, pair):
                dve.wait_ge(ht_hi_set, u.at + steps(pair + 1, NP))
                cols = slice(pair * 2 * P, (pair + 1) * 2 * P)
                v_.tensor_tensor(ht_lo[:, :, cols], ps_turn[pair][:, :].rearrange("p (k n) -> p k n", k=DT),
                                 ht_hi[:, :, cols], ALU.subtract).then_inc(ht_lo_set, steps(1, NP))

            def hidden_lo(u, k):
                if k == 0 and u.has_before():
                    dve.wait_ge(ff_done, u.at)
                dve.wait_ge(hid_hi_set, u.at + steps(k + 1, FT))
                count = steps(1 if k != VEC_LO[-1] else FT - VEC_LO[-1], FT)
                v_.tensor_tensor(hid_lo[:, k, :], hid[:, k % G_RING, :], hid_hi[:, k, :], ALU.subtract)\
                    .then_inc(hid_lo_vec, count)

            def residual2(u, pair):
                dve.wait_ge(ff_done, u.at + steps(pair + 1, NP))
                dve.wait_ge(h_b2_set, u.at + steps(2 * pair + 2, NT))
                if pair == 0 and u.has_before():
                    dve.wait_ge(normed2, u.at)
                for half in range(2):
                    t = 2 * pair + half
                    v_.tensor_tensor(y2[:, t, :], ps_acc[pair][:, half * D:(half + 1) * D], h_b2[:, t, :],
                                     ALU.add).then_inc(y2_set, steps(1, NT))

            def residual3(u):
                dve.wait_ge(x_first_in, at_last(u) + UNIT)
                for t in range(NT):
                    dve.wait_ge(x_new_set, u.at + steps(t + 1, NT))
                    v_.tensor_tensor(x_new[:, t, :], x_new[:, t, :], x_first[:, t, :], ALU.add)\
                        .then_inc(y3_set, steps(1, NT))

            dve.wait_ge(params_in, 16 * N_PARAMS)

            def slot(prev, u, v, w):
                if prev:
                    residual2(prev, 1)
                    moments(prev.at, 1, y2_set, y2, stats2, mv2, moments2)
                for k in range(FT):
                    if u and k in VEC_LO:
                        hidden_lo(u, k)
                    if w and 1 <= k <= NT:
                        dots(w, k - 1)
                    if v and k == 5:
                        prob_lo(v, 0)
                        prob_lo(v, 1)
                    if v and k == 6:
                        prob_lo(v, 2)
                        prob_lo(v, 3)
                if prev and last(prev):
                    residual3(prev)
                    for pair in range(NP):
                        moments(at_last(prev), pair, y3_set, x_new, stats3, mv3, moments3)
                if w:
                    for t in range(NT):
                        scores(w, t)
                    shifts(w)
                if v:
                    reciprocals(v)
                    residual1(v, 0)
                    moments(v.at, 0, y1_set, y1, stats1, mv1, moments1)
                    residual1(v, 1)
                    moments(v.at, 1, y1_set, y1, stats1, mv1, moments1)
                    affine1(v, 0)
                    affine1(v, 1)
                    h_lo(v, 0)
                    h_lo(v, 1)
                if u:
                    residual2(u, 0)
                    moments(u.at, 0, y2_set, y2, stats2, mv2, moments2)
                if w:
                    for t in range(NT):
                        probs(w, t)

            slots(dve, slot)


_INS = ["x", "adj", "L0_gnn_attn_w", "L0_gnn_attn_b", "L0_gnn_W1", "L0_gnn_b1", "L0_gnn_W2", "L0_gnn_b2",
        "L0_gnn_g1", "L0_gnn_beta1", "L0_gnn_g2", "L0_gnn_beta2"]


def kernel(**inputs):
    import numpy as _np
    import concourse.bacc as _bacc
    from concourse import mybir as _mybir
    from concourse.bass_utils import run_bass_kernel_spmd as _run

    nc = _bacc.Bacc("TRN2", target_bir_lowering=False, num_devices=1)
    arrays, args = {}, []
    for name in _INS:
        a = _np.ascontiguousarray(inputs[name])
        arrays[f"in_{name}"] = a
        args.append(nc.dram_tensor(f"in_{name}", a.shape, _mybir.dt.from_np(a.dtype), kind="ExternalInput").ap())
    out = nc.dram_tensor("out", inputs["x"].shape, _mybir.dt.float32, kind="ExternalOutput").ap()
    gnn_program(nc, *args, out)
    r = _run(nc, [arrays], core_ids=[0])
    return r.results[0]["out"]
```

```python
from contextlib import ExitStack

import concourse.bass as bass
from concourse import mybir

ALU = mybir.AluOpType
ACT = mybir.ActivationFunctionType
F32 = mybir.dt.float32
F32R = mybir.dt.float32r
BF16 = mybir.dt.bfloat16
I32 = mybir.dt.int32

P = 128
EPS = 1e-5
SLOPE = 0.2
BIG = 1e30
LOWEST = -3e38

UNIT = 16
F1_BANKS = 3
G_RING = 4
POOL_LO = (5,)
AGG_AFTER = (2, 4, 7, 7)


def steps(done, of):
    assert UNIT % of == 0
    return done * (UNIT // of)


class Unit:

    def __init__(self, layer, graph16, graphs):
        self.layer, self.graph16, self.graphs = layer, graph16, graphs
        self.at = graph16 + layer * graphs * UNIT

    def has_before(self, n=1):
        return not isinstance(self.at, int) or self.at >= n * UNIT

    def first_of_layer(self):
        return isinstance(self.graph16, int) and self.graph16 == 0

    def is_first(self):
        return isinstance(self.at, int) and self.at == 0


def gnn_program(nc, x, adj, attn_w, attn_b, w1, b1, w2, b2, g1, beta1, g2, beta2, out):
    B, N, D = x.shape
    L, _, F = w1.shape
    NT = N // P
    DT = D // P
    FT = F // P
    NP = NT // 2
    assert NT == 4 and 2 * D == 512 and N == 512 and UNIT % FT == 0

    x_mid = nc.dram_tensor("x_mid", [(L - 1) * B * P, NT * D], F32)
    x_rows = x.rearrange("b n d -> (b n) d")
    out_rows = out.rearrange("b n d -> (b n) d")
    adj_rows = adj.rearrange("b i j -> (b i) j")

    def node_rows(flat, first):
        return flat[bass.ds(first, N), :].rearrange("(t p) d -> p t d", p=P)

    with ExitStack() as ctx:
        def sb(name, shape, dt=F32):
            return ctx.enter_context(nc.sbuf_tensor(name, shape, dt))

        def psum(name):
            return ctx.enter_context(nc.psum_tensor(name, [P, 512], F32))

        def sem(name):
            return ctx.enter_context(nc.semaphore(name))

        ident = sb("ident", [P, P])
        eye_int = sb("eye_int", [P, P], I32)
        eps_t = sb("eps_t", [P, NT])
        neg_half = sb("neg_half", [P, NT])
        neg_one = sb("neg_one", [P, NT])
        zero_col = sb("zero_col", [P, 1])
        gelu_probe = sb("gelu_probe", [P, 1])
        attn_w_bc = sb("attn_w_bc", [P, L, 2, D])
        attn_b_bc = sb("attn_b_bc", [P, L])
        g1_bc = sb("g1_bc", [P, L, D])
        beta1_bc = sb("beta1_bc", [P, L, D])
        b2_bc = sb("b2_bc", [P, L, D])
        g2_bc = sb("g2_bc", [P, L, D])
        beta2_bc = sb("beta2_bc", [P, L, D])
        b1_col = sb("b1_col", [P, L, FT])
        w_stage = sb("w_stage", [P, DT * F])
        w1_hi = sb("w1_hi", [P, DT, F], F32R)
        w1_lo = sb("w1_lo", [P, DT, F], F32R)
        w2_hi = sb("w2_hi", [P, FT, D], F32R)
        w2_lo = sb("w2_lo", [P, FT, D], F32R)
        adj_t = sb("adj_t", [P, NT, N], I32)
        no_edge = sb("no_edge", [P, NT, N], BF16)
        x_t = sb("x_t", [P, NT, D])
        x_hi = sb("x_hi", [P, NT, D], F32R)
        x_lo = sb("x_lo", [P, NT, D], F32R)
        dot_junk = sb("dot_junk", [P, 4, D], BF16)
        s_i = sb("s_i", [P, NT])
        s_j = sb("s_j", [P, NT])
        row_max = sb("row_max", [P, NT])
        top = sb("top", [P, NT])
        top_leaky = sb("top_leaky", [P, NT])
        shift_pos = sb("shift_pos", [P, NT])
        shift_neg = sb("shift_neg", [P, NT])
        score = sb("score", [P, NT, N])
        prob = sb("prob", [P, NT, N])
        denom = sb("denom", [P, NT])
        x_res = sb("x_res", [P, NT, D])
        recip = sb("recip", [P, NT])
        pt_hi = sb("pt_hi", [P, NT, N], F32R)
        pt_lo = sb("pt_lo", [P, NT, N], F32R)
        y1 = sb("y1", [P, NT, D])
        stats1 = sb("stats1", [P, NT, 6])
        mv1 = sb("mv1", [P, NT, 2])
        var1 = sb("var1", [P, NT])
        rstd1 = sb("rstd1", [P, NT])
        h = sb("h", [P, NT, D])
        ht_hi = sb("ht_hi", [P, DT, N], F32R)
        ht_lo = sb("ht_lo", [P, DT, N], F32R)
        h_b2 = sb("h_b2", [P, NT, D])
        hid = sb("hid", [P, G_RING, N])
        hid_hi = sb("hid_hi", [P, FT, N], F32R)
        hid_lo = sb("hid_lo", [P, FT, N], F32R)
        y2 = sb("y2", [P, NT, D])
        stats2 = sb("stats2", [P, NT, 6])
        mv2 = sb("mv2", [P, NT, 2])
        var2 = sb("var2", [P, NT])
        rstd2 = sb("rstd2", [P, NT])
        mr2 = sb("mr2", [P, NT])
        nmr2 = sb("nmr2", [P, NT])
        x_new = sb("x_new", [P, NT, D])
        x_first = sb("x_first", [P, NT, D])
        stats3 = sb("stats3", [P, NT, 6])
        mv3 = sb("mv3", [P, NT, 2])
        var3 = sb("var3", [P, NT])
        rstd3 = sb("rstd3", [P, NT])
        mr3 = sb("mr3", [P, NT])
        nmr3 = sb("nmr3", [P, NT])

        ps_hid = [psum(f"ps_hid{i}") for i in range(F1_BANKS)]
        ps_turn = [psum(f"ps_turn{i}") for i in range(2)]
        ps_acc = [psum(f"ps_acc{i}") for i in range(NP)]
        ps_sj = psum("ps_sj")

        attn_in = [sem(f"attn_in{layer}") for layer in range(L)]
        b1_in = sem("b1_in")
        params_in = [sem(f"params_in{layer}") for layer in range(L)]
        consts_set = sem("consts_set")
        ident_set = sem("ident_set")
        w_in = sem("w_in")
        w_hi_set = sem("w_hi_set")
        w_lo_set = sem("w_lo_set")
        adj_in = sem("adj_in")
        x_in = sem("x_in")
        x_res_in = sem("x_res_in")
        x_first_in = sem("x_first_in")
        stored = sem("stored")
        diag_set = sem("diag_set")
        masked = sem("masked")
        dotted = sem("dotted")
        spread = sem("spread")
        scored = sem("scored")
        shifted = sem("shifted")
        exped = sem("exped")
        prob_set = sem("prob_set")
        x_hi_set = sem("x_hi_set")
        x_lo_set = sem("x_lo_set")
        turned = sem("turned")
        pt_hi_set = sem("pt_hi_set")
        pt_lo_set = sem("pt_lo_set")
        recip_set = sem("recip_set")
        agg_done = sem("agg_done")
        y1_set = sem("y1_set")
        moments1 = sem("moments1")
        rstd1_set = sem("rstd1_set")
        centered1 = sem("centered1")
        h_set = sem("h_set")
        h_turned = sem("h_turned")
        ht_hi_set = sem("ht_hi_set")
        ht_lo_set = sem("ht_lo_set")
        h_b2_set = sem("h_b2_set")
        gelu_ready = sem("gelu_ready")
        hid_done = sem("hid_done")
        hid_set = sem("hid_set")
        hid_hi_set = sem("hid_hi_set")
        hid_lo_vec = sem("hid_lo_vec")
        hid_lo_pool = sem("hid_lo_pool")
        ff_done = sem("ff_done")
        y2_set = sem("y2_set")
        moments2 = sem("moments2")
        rstd2_set = sem("rstd2_set")
        normed2 = sem("normed2")
        scaled2 = sem("scaled2")
        x_new_set = sem("x_new_set")
        y3_set = sem("y3_set")
        moments3 = sem("moments3")
        rstd3_set = sem("rstd3_set")
        normed3 = sem("normed3")

        VEC_LO = [k for k in range(FT) if k not in POOL_LO]
        N_PARAMS = 5

        def last(u):
            return u.layer == L - 1

        def at_last(u):
            return u.graph16

        def slots(eng, slot):
            def unit(i):
                return Unit(i // B, i % B * UNIT, B) if 0 <= i < L * B else None

            def peeled(i):
                slot(unit(i - 2), unit(i - 1), unit(i), unit(i + 1), unit(i + 2))

            peeled(-2)
            peeled(-1)
            for layer in range(L):
                peeled(layer * B)
                peeled(layer * B + 1)
                with eng.Fori(2, B - 2) as graph:
                    slot(*(Unit(layer, (graph + k) * UNIT, B) for k in (-2, -1, 0, 1, 2)))
                peeled(layer * B + B - 2)
                peeled(layer * B + B - 1)
            peeled(L * B)
            peeled(L * B + 1)

        block = ctx.enter_context(nc.Block())

        @block.sync
        def _(sp):
            def load_weights(n):
                if n:
                    sp.wait_ge(w_hi_set, n)
                    sp.wait_ge(w_lo_set, n)
                layer, second = divmod(n, 2)
                w, k = (w2, FT) if second else (w1, DT)
                sp.dma_start(w_stage[:, :].rearrange("p (k f) -> p k f", k=k),
                             w[layer].rearrange("(k p) f -> p k f", p=P)).then_inc(w_in, 16)

            def known(value):
                return value if isinstance(value, int) else sp.snap(sp.to_reg(value))

            def source_of_x(u):
                if u.layer == 0:
                    return node_rows(x_rows, known(u.graph16 * (N // UNIT))), None
                here = known(u.graph16 * (P // UNIT) + (u.layer - 1) * B * P)
                return x_mid[bass.ds(here, P), :], known(u.at + UNIT - B * UNIT)

            def load_x(tile, source, layer_before, signal):
                if layer_before is not None:
                    sp.wait_ge(stored, layer_before)
                    sp.dma_start(tile[:, :, :].rearrange("p t d -> p (t d)"), source).then_inc(signal, 16)
                else:
                    sp.dma_start(tile[:, :, :], source).then_inc(signal, 16)

            def load_prepare(u):
                source, layer_before = source_of_x(u)
                adj_source = node_rows(adj_rows, known(u.graph16 * (N // UNIT)))
                at = known(u.at)
                if u.has_before():
                    sp.wait_ge(masked, at)
                sp.dma_start(adj_t[:, :, :], adj_source).then_inc(adj_in, 16)
                if u.has_before():
                    sp.wait_ge(dotted, at)
                    sp.wait_ge(x_lo_set, at)
                load_x(x_t, source, layer_before, x_in)

            def load_residual(u):
                source, layer_before = source_of_x(u)
                at = known(u.at)
                if u.has_before():
                    sp.wait_ge(y1_set, at)
                load_x(x_res, source, layer_before, x_res_in)

            def load_first(u):
                source = node_rows(x_rows, known(u.graph16 * (N // UNIT)))
                if not u.first_of_layer():
                    sp.wait_ge(stored, known(u.at))
                sp.dma_start(x_first[:, :, :], source).then_inc(x_first_in, 16)

            def store(u):
                at = known(u.at)
                if last(u):
                    ready, full, tile = normed3, known(at_last(u) + UNIT), x_first[:, :, :]
                    target = node_rows(out_rows, known(u.graph16 * (N // UNIT)))
                else:
                    ready, full = x_new_set, known(u.at + UNIT)
                    tile = x_new[:, :, :].rearrange("p t d -> p (t d)")
                    target = x_mid[bass.ds(known(u.graph16 * (P // UNIT) + u.layer * B * P), P), :]
                if u.has_before():
                    sp.wait_ge(stored, at)
                sp.wait_ge(ready, full)
                sp.dma_start(target, tile).then_inc(stored, 16)

            def load_attn(layer):
                sp.dma_start(attn_w_bc[:, layer, :, :].rearrange("p s d -> p (s d)"),
                             attn_w[layer].partition_broadcast(P)).then_inc(attn_in[layer], 16)

            def load_params(layer):
                for tile, param in ((g1_bc, g1), (beta1_bc, beta1), (b2_bc, b2), (g2_bc, g2), (beta2_bc, beta2)):
                    sp.dma_start(tile[:, layer, :], param[layer].partition_broadcast(P))\
                        .then_inc(params_in[layer], 16)

            load_attn(0)
            sp.dma_start(attn_b_bc[:, :], attn_b.partition_broadcast(P)).then_inc(attn_in[0], 16)
            load_prepare(Unit(0, 0, B))
            load_weights(0)
            load_params(0)
            with nc.allow_non_contiguous_dma(reason="b1 by partition, once"):
                sp.dma_start(b1_col[:, :, :], b1.rearrange("l (k p) -> p l k", p=P)).then_inc(b1_in, 16)

            def slot(old, prev, u, v, w):
                if u and u.first_of_layer():
                    load_weights(2 * u.layer + 1)
                if w and not w.is_first():
                    load_prepare(w)
                if v:
                    load_residual(v)
                if u and u.is_first():
                    for layer in range(1, L):
                        load_attn(layer)
                        load_params(layer)
                if old and last(old):
                    store(old)
                if prev and last(prev):
                    load_first(prev)
                elif prev:
                    store(prev)
                if u and u.first_of_layer() and u.layer + 1 < L:
                    load_weights(2 * u.layer + 2)

            slots(sp, slot)
            sp.wait_ge(stored, L * B * UNIT)

        @block.gpsimd
        def _(pool):
            tt = nc.gpsimd.tensor_tensor

            def self_loops(u):
                for t in range(NT):
                    if t == 0:
                        pool.wait_ge(adj_in, u.at + UNIT)
                    blk = adj_t[:, t, t * P:(t + 1) * P]
                    tt(blk, blk, eye_int[:, :], ALU.add).then_inc(diag_set, steps(1, NT))

            def split_x(u):
                pool.wait_ge(x_hi_set, u.at + UNIT)
                tt(x_lo[:, :, :], x_t[:, :, :], x_hi[:, :, :], ALU.subtract).then_inc(x_lo_set, UNIT)

            def rstd_of(u_at, pair, moments, mv, var, rstd, signal, of):
                s = slice(2 * pair, 2 * pair + 2)
                pool.wait_ge(moments, u_at + steps(4 * pair + 4, 8))
                tt(var[:, s], mv[:, s, 1], eps_t[:, s], ALU.add).then_inc(signal, steps(1, of))
                pool.wait_ge(signal, u_at + steps((pair * of) // 2 + 1, of))
                tt(rstd[:, s], var[:, s], neg_half[:, s], ALU.pow).then_inc(signal, steps(1, of))

            def offset_of(u_at, pair, mv, rstd, mr, nmr, signal):
                s = slice(2 * pair, 2 * pair + 2)
                pool.wait_ge(signal, u_at + steps(4 * pair + 2, 8))
                tt(mr[:, s], mv[:, s, 0], rstd[:, s], ALU.mult).then_inc(signal, steps(1, 8))
                pool.wait_ge(signal, u_at + steps(4 * pair + 3, 8))
                tt(nmr[:, s], mr[:, s], neg_one[:, s], ALU.mult).then_inc(signal, steps(1, 8))

            def add_b2(u):
                if u.first_of_layer():
                    pool.wait_ge(params_in[u.layer], 16 * N_PARAMS)
                if u.has_before():
                    pool.wait_ge(y2_set, u.at)
                for t in range(NT):
                    pool.wait_ge(h_set, u.at + steps(t + 1, NT))
                    tt(h_b2[:, t, :], h[:, t, :], b2_bc[:, u.layer, :], ALU.add).then_inc(h_b2_set, steps(1, NT))

            def affine2(u):
                for t in range(NT):
                    pool.wait_ge(normed2, u.at + steps(t + 1, NT))
                    tt(x_new[:, t, :], x_new[:, t, :], g2_bc[:, u.layer, :], ALU.mult)\
                        .then_inc(scaled2, steps(1, NT))
                for t in range(NT):
                    pool.wait_ge(scaled2, u.at + steps(t + 1, NT))
                    tt(x_new[:, t, :], x_new[:, t, :], beta2_bc[:, u.layer, :], ALU.add)\
                        .then_inc(x_new_set, steps(1, NT))

            def residual3(u):
                pool.wait_ge(x_first_in, at_last(u) + UNIT)
                for t in range(NT):
                    pool.wait_ge(x_new_set, u.at + steps(t + 1, NT))
                    tt(x_first[:, t, :], x_new[:, t, :], x_first[:, t, :], ALU.add)\
                        .then_inc(y3_set, steps(1, NT))

            def hidden_lo(u, n):
                k = POOL_LO[n]
                if n == 0 and u.has_before():
                    pool.wait_ge(ff_done, u.at)
                pool.wait_ge(hid_hi_set, u.at + steps(k + 1, FT))
                tt(hid_lo[:, k, :], hid[:, k % G_RING, :], hid_hi[:, k, :], ALU.subtract)\
                    .then_inc(hid_lo_pool, steps(1, len(POOL_LO)))

            nc.gpsimd.memset(ident[:, :], 0.0).then_inc(ident_set, 1)
            nc.gpsimd.memset(eye_int[:, :], 0).then_inc(ident_set, 1)
            nc.gpsimd.memset(eps_t[:, :], EPS).then_inc(consts_set, 1)
            nc.gpsimd.memset(neg_half[:, :], -0.5).then_inc(consts_set, 1)
            nc.gpsimd.memset(neg_one[:, :], -1.0).then_inc(consts_set, 1)
            nc.gpsimd.memset(zero_col[:, :], 0.0).then_inc(consts_set, 1)
            pool.wait_ge(ident_set, 2)
            nc.gpsimd.affine_select(out=ident[:, :], in_=ident[:, :], compare_op=ALU.not_equal, fill=1.0,
                                    base=0, pattern=[[-1, P]], channel_multiplier=1).then_inc(ident_set, 1)
            pool.wait_ge(ident_set, 3)
            nc.gpsimd.tensor_copy(eye_int[:, :], ident[:, :]).then_inc(ident_set, 1)
            pool.wait_ge(ident_set, 4)
            pool.wait_ge(consts_set, 4)

            def slot(old, prev, u, v, w):
                if prev:
                    rstd_of(prev.at, 0, moments2, mv2, var2, rstd2, rstd2_set, 8)
                    offset_of(prev.at, 0, mv2, rstd2, mr2, nmr2, rstd2_set)
                if w:
                    self_loops(w)
                if prev:
                    rstd_of(prev.at, 1, moments2, mv2, var2, rstd2, rstd2_set, 8)
                    offset_of(prev.at, 1, mv2, rstd2, mr2, nmr2, rstd2_set)
                if u:
                    add_b2(u)
                if old and last(old):
                    for pair in range(NP):
                        rstd_of(at_last(old), pair, moments3, mv3, var3, rstd3, rstd3_set, 8)
                        offset_of(at_last(old), pair, mv3, rstd3, mr3, nmr3, rstd3_set)
                if prev:
                    affine2(prev)
                if u:
                    for n in range(len(POOL_LO)):
                        hidden_lo(u, n)
                if v:
                    rstd_of(v.at, 0, moments1, mv1, var1, rstd1, rstd1_set, 4)
                    rstd_of(v.at, 1, moments1, mv1, var1, rstd1, rstd1_set, 4)
                if w:
                    split_x(w)
                if prev and last(prev):
                    residual3(prev)

            slots(pool, slot)

        @block.scalar
        def _(act):
            def weight_hi(n):
                hi, k = (w2_hi, FT) if n % 2 else (w1_hi, DT)
                act.wait_ge(w_in, 16 * (n + 1))
                if n > 1:
                    act.wait_ge(ff_done if n % 2 else hid_done, n // 2 * B * UNIT)
                nc.scalar.activation(hi[:, :, :], w_stage[:, :].rearrange("p (k f) -> p k f", k=k), ACT.Copy)\
                    .then_inc(w_hi_set, 1)

            def mask(u):
                act.wait_ge(diag_set, u.at + UNIT)
                if u.has_before():
                    act.wait_ge(scored, u.at)
                nc.scalar.activation(no_edge[:, :, :], adj_t[:, :, :], ACT.Relu, bias=BIG, scale=-BIG)\
                    .then_inc(masked, UNIT)

            def exps(u, pair):
                if pair == 0:
                    act.wait_ge(shifted, u.at + UNIT)
                    if u.has_before():
                        act.wait_ge(turned, u.at)
                for t in (2 * pair, 2 * pair + 1):
                    nc.scalar.activation(prob[:, t, :], score[:, t, :], ACT.Exp, bias=shift_pos[:, t:t + 1])\
                        .then_inc(exped, steps(1, 2 * NT))
                for t in (2 * pair, 2 * pair + 1):
                    act.wait_ge(exped, u.at + steps(2 * pair + t + 1, 2 * NT))
                    nc.scalar.activation(score[:, t, :], score[:, t, :], ACT.Exp, bias=shift_neg[:, t:t + 1],
                                         scale=SLOPE).then_inc(exped, steps(1, 2 * NT))

            def split_x(u):
                act.wait_ge(x_in, u.at + UNIT)
                if u.has_before():
                    act.wait_ge(agg_done, u.at)
                nc.scalar.activation(x_hi[:, :, :], x_t[:, :, :], ACT.Copy).then_inc(x_hi_set, UNIT)

            def prob_hi(u, jt):
                if jt == 0 and u.has_before():
                    act.wait_ge(agg_done, u.at)
                act.wait_ge(turned, u.at + steps(jt + 1, NT))
                nc.scalar.activation(pt_hi[:, jt, :], ps_turn[jt % 2][:, :], ACT.Copy)\
                    .then_inc(pt_hi_set, steps(1, NT))

            def h_hi(u, pair):
                if pair == 0 and u.has_before():
                    act.wait_ge(hid_done, u.at)
                act.wait_ge(h_turned, u.at + steps(pair + 1, NP))
                nc.scalar.activation(ht_hi[:, :, pair * 2 * P:(pair + 1) * 2 * P],
                                     ps_turn[pair][:, :].rearrange("p (k n) -> p k n", k=DT), ACT.Copy)\
                    .then_inc(ht_hi_set, steps(1, NP))

            def gelu(u, k):
                if k >= G_RING or u.has_before():
                    free = k - G_RING
                    back = u.at if free >= 0 else u.at - UNIT
                    free %= FT
                    if free in POOL_LO:
                        act.wait_ge(hid_lo_pool, back + steps(POOL_LO.index(free) + 1, len(POOL_LO)))
                    else:
                        act.wait_ge(hid_lo_vec, back + steps(free + 1, FT))
                act.wait_ge(hid_done, u.at + steps(k + 1, FT))
                if k == 0 and u.is_first():
                    act.wait_ge(b1_in, 16)
                nc.scalar.activation(hid[:, k % G_RING, :], ps_hid[k % F1_BANKS][:, :], ACT.Gelu,
                                     bias=b1_col[:, u.layer, k:k + 1]).then_inc(hid_set, steps(1, FT))

            def hidden_hi(u, k):
                if k == 0 and u.has_before():
                    act.wait_ge(ff_done, u.at)
                act.wait_ge(hid_set, u.at + steps(k + 1, FT))
                nc.scalar.activation(hid_hi[:, k, :], hid[:, k % G_RING, :], ACT.Copy)\
                    .then_inc(hid_hi_set, steps(1, FT))

            def normalize2(u, pair):
                act.wait_ge(rstd2_set, u.at + steps(4 * pair + 4, 8))
                if pair == 0 and last(u) and not u.first_of_layer():
                    act.wait_ge(y3_set, at_last(u))
                elif pair == 0 and u.has_before():
                    act.wait_ge(stored, u.at)
                for t in (2 * pair, 2 * pair + 1):
                    nc.scalar.activation(x_new[:, t, :], y2[:, t, :], ACT.Identity, bias=nmr2[:, t:t + 1],
                                         scale=rstd2[:, t:t + 1]).then_inc(normed2, steps(1, NT))

            def normalize3(u, pair):
                act.wait_ge(rstd3_set, at_last(u) + steps(4 * pair + 4, 8))
                for t in (2 * pair, 2 * pair + 1):
                    nc.scalar.activation(x_first[:, t, :], x_first[:, t, :], ACT.Identity, bias=nmr3[:, t:t + 1],
                                         scale=rstd3[:, t:t + 1]).then_inc(normed3, steps(1, NT))

            def load_gelu_table(u):
                if u.has_before():
                    act.wait_ge(gelu_ready, u.at)
                nc.scalar.activation(gelu_probe[:, :], zero_col[:, :], ACT.Gelu).then_inc(gelu_ready, UNIT)

            act.wait_ge(consts_set, 4)

            def slot(old, prev, u, v, w):
                if v:
                    prob_hi(v, 0)
                    prob_hi(v, 1)
                for k in range(FT):
                    if u:
                        gelu(u, k)
                    if v and k == 0:
                        prob_hi(v, 2)
                        prob_hi(v, 3)
                    if u and k > 0:
                        hidden_hi(u, k - 1)
                    if w and k == 2:
                        mask(w)
                    if prev and k in (4, 5):
                        normalize2(prev, k - 4)
                    if old and last(old) and k in (6, 7):
                        normalize3(old, k - 6)
                    if u and u.first_of_layer() and k == 5:
                        weight_hi(2 * u.layer + 1)
                if u:
                    hidden_hi(u, FT - 1)
                if v and v.first_of_layer():
                    weight_hi(2 * v.layer)
                if w:
                    split_x(w)
                    for pair in range(NP):
                        exps(w, pair)
                if v:
                    h_hi(v, 0)
                    h_hi(v, 1)
                    load_gelu_table(v)

            slots(act, slot)

        @block.tensor
        def _(pe):
            def hidden(u, k):
                if k == 0:
                    pe.wait_ge(ht_lo_set, u.at + UNIT)
                    if u.first_of_layer():
                        pe.wait_ge(w_lo_set, 2 * u.layer + 1)
                if k >= F1_BANKS or u.has_before():
                    free = k - F1_BANKS
                    if free < 0:
                        free = max(j for j in range(FT) if j % F1_BANKS == k) - FT
                    pe.wait_ge(hid_set, u.at + steps(free + 1, FT))
                cols = slice(k * P, (k + 1) * P)
                terms = [(w, ht, d) for d in range(DT) for w, ht in ((w1_hi, ht_hi), (w1_hi, ht_lo), (w1_lo, ht_hi))]
                for n, (w, ht, d) in enumerate(terms):
                    mm = nc.tensor.matmul(ps_hid[k % F1_BANKS][:, :], w[:, d, cols], ht[:, d, :],
                                          start=(n == 0), stop=(n == len(terms) - 1))
                mm.then_inc(hid_done, steps(1, FT))

            def turn_prob(u, jt):
                if jt == 0:
                    pe.wait_ge(prob_set, u.at + UNIT)
                if jt >= 2:
                    pe.wait_ge(pt_lo_set, u.at + steps(jt - 1, NT))
                elif u.has_before():
                    pe.wait_ge(ht_lo_set, u.at - UNIT + steps(jt + 1, NP))
                for it in range(NT):
                    mm = nc.tensor.transpose(ps_turn[jt % 2][:, it * P:(it + 1) * P],
                                             prob[:, it, jt * P:(jt + 1) * P], ident[:, :])
                mm.then_inc(turned, steps(1, NT))

            def spread_sj(u):
                pe.wait_ge(dotted, u.at + UNIT)
                if u.has_before():
                    pe.wait_ge(scored, u.at)
                for t in range(NT):
                    mm = nc.tensor.matmul(ps_sj[:, t * P:(t + 1) * P], s_j[:, t:t + 1].to_broadcast([P, P]),
                                          ident[:, :], start=True, stop=True)
                mm.then_inc(spread, UNIT)

            def aggregate(u, t):
                pair, half = divmod(t, 2)
                if t == 0:
                    pe.wait_ge(pt_lo_set, u.at + UNIT)
                    pe.wait_ge(x_lo_set, u.at + UNIT)
                if half == 0 and u.has_before(2):
                    pe.wait_ge(y2_set, u.at - 2 * UNIT + steps(2 * pair + 2, NT))
                cols = slice(t * P, (t + 1) * P)
                terms = [(p, xs, jt) for jt in range(NT)
                         for p, xs in ((pt_hi, x_hi), (pt_hi, x_lo), (pt_lo, x_hi))]
                for n, (p, xs, jt) in enumerate(terms):
                    mm = nc.tensor.matmul(ps_acc[pair][:, half * D:(half + 1) * D], p[:, jt, cols],
                                          xs[:, jt, :], start=(n == 0), stop=(n == len(terms) - 1))
                if half:
                    mm.then_inc(agg_done, steps(1, NP))

            def feed(u, t, next_unit):
                pair, half = divmod(t, 2)
                if t == 0 and u.first_of_layer():
                    pe.wait_ge(w_lo_set, 2 * u.layer + 2)
                if half == 0 and next_unit:
                    pe.wait_ge(y1_set, next_unit.at + steps(2 * pair + 2, NT))
                cols = slice(t * P, (t + 1) * P)
                terms = [(g, w, k) for k in VEC_LO + list(POOL_LO)
                         for g, w in ((hid_hi, w2_hi), (hid_hi, w2_lo), (hid_lo, w2_hi))]
                for n, (g, w, k) in enumerate(terms):
                    if t == 0 and n % 3 == 0:
                        if k in POOL_LO:
                            pe.wait_ge(hid_lo_pool, u.at + steps(POOL_LO.index(k) + 1, len(POOL_LO)))
                        else:
                            pe.wait_ge(hid_lo_vec, u.at + steps(k + 1, FT))
                    mm = nc.tensor.matmul(ps_acc[pair][:, half * D:(half + 1) * D], g[:, k, cols], w[:, k, :],
                                          start=(n == 0), stop=(n == len(terms) - 1))
                if half:
                    mm.then_inc(ff_done, steps(1, NP))

            def turn_h(u, pair):
                pe.wait_ge(h_set, u.at + steps(2 * pair + 2, NT))
                pe.wait_ge(pt_lo_set, u.at + steps(pair + 3, NT))
                for d in range(DT):
                    for half in range(2):
                        mm = nc.tensor.transpose(ps_turn[pair][:, (2 * d + half) * P:(2 * d + half + 1) * P],
                                                 h[:, 2 * pair + half, d * P:(d + 1) * P], ident[:, :])
                mm.then_inc(h_turned, steps(1, NP))

            pe.wait_ge(ident_set, 3)

            def slot(old, prev, u, v, w):
                if v:
                    turn_prob(v, 0)
                    turn_prob(v, 1)
                for k in range(FT):
                    if u:
                        hidden(u, k)
                    if v and k == 0:
                        turn_prob(v, 2)
                        turn_prob(v, 3)
                    for t in range(NT):
                        if v and AGG_AFTER[t] == k:
                            aggregate(v, t)
                    if w and k == 5:
                        spread_sj(w)
                if u:
                    feed(u, 0, v)
                    feed(u, 1, v)
                if v:
                    turn_h(v, 0)
                if u:
                    feed(u, 2, v)
                if v:
                    turn_h(v, 1)
                if u:
                    feed(u, 3, v)

            slots(pe, slot)

        @block.vector
        def _(dve):
            v_ = nc.vector

            def dots(u, t):
                if t == 0:
                    if u.first_of_layer():
                        dve.wait_ge(attn_in[u.layer], 16 if u.layer else 32)
                    dve.wait_ge(x_in, u.at + UNIT)
                    if u.has_before():
                        dve.wait_ge(spread, u.at)
                        dve.wait_ge(prob_set, u.at)
                elif t >= 2:
                    dve.wait_ge(dotted, u.at + steps(2 * t - 2, 2 * NT))
                v_.tensor_tensor_reduce(dot_junk[:, 2 * t % 4, :], x_t[:, t, :], attn_w_bc[:, u.layer, 0, :],
                                        1.0, attn_b_bc[:, u.layer:u.layer + 1], ALU.mult, ALU.add,
                                        s_i[:, t:t + 1]).then_inc(dotted, steps(1, 2 * NT))
                v_.tensor_tensor_reduce(dot_junk[:, (2 * t + 1) % 4, :], x_t[:, t, :], attn_w_bc[:, u.layer, 1, :],
                                        1.0, 0.0, ALU.mult, ALU.add,
                                        s_j[:, t:t + 1]).then_inc(dotted, steps(1, 2 * NT))

            def scores(u, t):
                if t == 0:
                    dve.wait_ge(spread, u.at + UNIT)
                    dve.wait_ge(masked, u.at + UNIT)
                v_.tensor_tensor_reduce(score[:, t, :], ps_sj[:, :], no_edge[:, t, :], 1.0, LOWEST,
                                        ALU.subtract, ALU.max, row_max[:, t:t + 1])\
                    .then_inc(scored, steps(1, NT))

            def shifts(u):
                dve.wait_ge(scored, u.at + UNIT)
                v_.tensor_tensor(top[:, :], row_max[:, :], s_i[:, :], ALU.add).then_inc(shifted, steps(1, 4))
                dve.wait_ge(shifted, u.at + steps(1, 4))
                v_.scalar_tensor_tensor(out=top_leaky[:, :], in0=top[:, :], scalar=SLOPE, in1=top[:, :],
                                        op0=ALU.mult, op1=ALU.max).then_inc(shifted, steps(1, 4))
                dve.wait_ge(shifted, u.at + steps(2, 4))
                v_.tensor_tensor(shift_pos[:, :], s_i[:, :], top_leaky[:, :], ALU.subtract)\
                    .then_inc(shifted, steps(1, 4))
                v_.scalar_tensor_tensor(out=shift_neg[:, :], in0=s_i[:, :], scalar=SLOPE, in1=top_leaky[:, :],
                                        op0=ALU.mult, op1=ALU.subtract).then_inc(shifted, steps(1, 4))

            def probs(u, t):
                dve.wait_ge(exped, u.at + steps(t + 3 + 2 * (t // 2), 2 * NT))
                v_.scalar_tensor_tensor(out=prob[:, t, :], in0=prob[:, t, :], scalar=1.0, in1=score[:, t, :],
                                        op0=ALU.mult, op1=ALU.max, accum_out=denom[:, t:t + 1])\
                    .then_inc(prob_set, steps(1, NT))

            def prob_lo(u, jt):
                if jt == 0 and u.has_before():
                    dve.wait_ge(agg_done, u.at)
                dve.wait_ge(pt_hi_set, u.at + steps(jt + 1, NT))
                v_.tensor_tensor(pt_lo[:, jt, :], ps_turn[jt % 2][:, :], pt_hi[:, jt, :], ALU.subtract)\
                    .then_inc(pt_lo_set, steps(1, NT))

            def reciprocals(u):
                dve.wait_ge(prob_set, u.at + UNIT)
                v_.reciprocal(recip[:, :], denom[:, :]).then_inc(recip_set, UNIT)

            def residual1(u, pair):
                dve.wait_ge(agg_done, u.at + steps(pair + 1, NP))
                if pair == 0:
                    dve.wait_ge(recip_set, u.at + UNIT)
                    dve.wait_ge(x_res_in, u.at + UNIT)
                for half in range(2):
                    t = 2 * pair + half
                    v_.scalar_tensor_tensor(out=y1[:, t, :], in0=ps_acc[pair][:, half * D:(half + 1) * D],
                                            scalar=recip[:, t:t + 1], in1=x_res[:, t, :],
                                            op0=ALU.mult, op1=ALU.add).then_inc(y1_set, steps(1, NT))

            def moments(at, pair, ready, y, stats, mv, signal):
                for half in range(2):
                    t = 2 * pair + half
                    dve.wait_ge(ready, at + steps(t + 1, NT))
                    v_.bn_stats(stats[:, t, :], y[:, t, :]).then_inc(signal, steps(1, 8))
                for half in range(2):
                    t = 2 * pair + half
                    dve.wait_ge(signal, at + steps(4 * pair + 1 + half, 8))
                    v_.bn_aggr(mv[:, t, :], stats[:, t, :]).then_inc(signal, steps(1, 8))

            def affine1(u, pair):
                if pair == 0 and u.first_of_layer():
                    dve.wait_ge(params_in[u.layer], 16 * N_PARAMS)
                dve.wait_ge(rstd1_set, u.at + steps(2 * pair + 2, 4))
                if pair == 0 and u.has_before():
                    dve.wait_ge(h_turned, u.at)
                    dve.wait_ge(h_b2_set, u.at)
                for t in (2 * pair, 2 * pair + 1):
                    v_.scalar_tensor_tensor(out=h[:, t, :], in0=y1[:, t, :], scalar=mv1[:, t, 0:1],
                                            in1=g1_bc[:, u.layer, :], op0=ALU.subtract, op1=ALU.mult)\
                        .then_inc(centered1, steps(1, NT))
                for t in (2 * pair, 2 * pair + 1):
                    dve.wait_ge(centered1, u.at + steps(t + 1, NT))
                    v_.scalar_tensor_tensor(out=h[:, t, :], in0=h[:, t, :], scalar=rstd1[:, t:t + 1],
                                            in1=beta1_bc[:, u.layer, :], op0=ALU.mult, op1=ALU.add)\
                        .then_inc(h_set, steps(1, NT))

            def h_lo(u, pair):
                dve.wait_ge(ht_hi_set, u.at + steps(pair + 1, NP))
                cols = slice(pair * 2 * P, (pair + 1) * 2 * P)
                v_.tensor_tensor(ht_lo[:, :, cols], ps_turn[pair][:, :].rearrange("p (k n) -> p k n", k=DT),
                                 ht_hi[:, :, cols], ALU.subtract).then_inc(ht_lo_set, steps(1, NP))

            def hidden_lo(u, k):
                if k == 0 and u.has_before():
                    dve.wait_ge(ff_done, u.at)
                dve.wait_ge(hid_hi_set, u.at + steps(k + 1, FT))
                following = min([j for j in VEC_LO if j > k] + [FT])
                v_.tensor_tensor(hid_lo[:, k, :], hid[:, k % G_RING, :], hid_hi[:, k, :], ALU.subtract)\
                    .then_inc(hid_lo_vec, steps(following - k, FT))

            def residual2(u, pair):
                dve.wait_ge(ff_done, u.at + steps(pair + 1, NP))
                dve.wait_ge(h_b2_set, u.at + steps(2 * pair + 2, NT))
                if pair == 0 and u.has_before():
                    dve.wait_ge(normed2, u.at)
                for half in range(2):
                    t = 2 * pair + half
                    v_.tensor_tensor(y2[:, t, :], ps_acc[pair][:, half * D:(half + 1) * D], h_b2[:, t, :],
                                     ALU.add).then_inc(y2_set, steps(1, NT))

            def weight_lo(n):
                hi, lo, k = (w2_hi, w2_lo, FT) if n % 2 else (w1_hi, w1_lo, DT)
                dve.wait_ge(w_hi_set, n + 1)
                v_.tensor_tensor(lo[:, :, :], w_stage[:, :].rearrange("p (k f) -> p k f", k=k), hi[:, :, :],
                                 ALU.subtract).then_inc(w_lo_set, 1)

            def slot(old, prev, u, v, w):
                if v:
                    prob_lo(v, 0)
                    prob_lo(v, 1)
                if prev:
                    residual2(prev, 1)
                    moments(prev.at, 1, y2_set, y2, stats2, mv2, moments2)
                if v:
                    prob_lo(v, 2)
                    prob_lo(v, 3)
                for k in range(FT):
                    if u and k in VEC_LO:
                        hidden_lo(u, k)
                    if w and k in (1, 2):
                        dots(w, 2 * k - 2)
                        dots(w, 2 * k - 1)
                    if old and last(old) and k == 0:
                        for pair in range(NP):
                            moments(at_last(old), pair, y3_set, x_first, stats3, mv3, moments3)
                    if v and k == 5:
                        reciprocals(v)
                        residual1(v, 0)
                    if w and k in (5, 6):
                        scores(w, 2 * k - 10)
                        scores(w, 2 * k - 9)
                if w:
                    shifts(w)
                if v:
                    moments(v.at, 0, y1_set, y1, stats1, mv1, moments1)
                    residual1(v, 1)
                    moments(v.at, 1, y1_set, y1, stats1, mv1, moments1)
                if u and u.first_of_layer():
                    weight_lo(2 * u.layer + 1)
                if v:
                    affine1(v, 0)
                    affine1(v, 1)
                if v and v.first_of_layer():
                    weight_lo(2 * v.layer)
                if w:
                    probs(w, 0)
                    probs(w, 1)
                if v:
                    h_lo(v, 0)
                if w:
                    probs(w, 2)
                    probs(w, 3)
                if u:
                    residual2(u, 0)
                    moments(u.at, 0, y2_set, y2, stats2, mv2, moments2)
                if v:
                    h_lo(v, 1)

            slots(dve, slot)


_INS = ["x", "adj", "L0_gnn_attn_w", "L0_gnn_attn_b", "L0_gnn_W1", "L0_gnn_b1", "L0_gnn_W2", "L0_gnn_b2",
        "L0_gnn_g1", "L0_gnn_beta1", "L0_gnn_g2", "L0_gnn_beta2"]


def kernel(**inputs):
    import numpy as _np
    import concourse.bacc as _bacc
    from concourse import mybir as _mybir
    from concourse.bass_utils import run_bass_kernel_spmd as _run

    nc = _bacc.Bacc("TRN2", target_bir_lowering=False, num_devices=1)
    arrays, args = {}, []
    for name in _INS:
        a = _np.ascontiguousarray(inputs[name])
        arrays[f"in_{name}"] = a
        args.append(nc.dram_tensor(f"in_{name}", a.shape, _mybir.dt.from_np(a.dtype), kind="ExternalInput").ap())
    out = nc.dram_tensor("out", inputs["x"].shape, _mybir.dt.float32, kind="ExternalOutput").ap()
    gnn_program(nc, *args, out)
    r = _run(nc, [arrays], core_ids=[0])
    return r.results[0]["out"]
```

```python
from contextlib import ExitStack

import concourse.bass as bass
from concourse import mybir

ALU = mybir.AluOpType
ACT = mybir.ActivationFunctionType
F32 = mybir.dt.float32
F32R = mybir.dt.float32r
BF16 = mybir.dt.bfloat16
I32 = mybir.dt.int32

P = 128
EPS = 1e-5
SLOPE = 0.2
BIG = 1e30
LOWEST = -3e38

UNIT = 16
F1_BANKS = 3
G_RING = 4
POOL_LO = (2, 5)
AGG_AFTER = (2, 3, 7, 7)


def steps(done, of):
    assert UNIT % of == 0
    return done * (UNIT // of)


class Unit:

    def __init__(self, layer, graph16, parity, graphs):
        self.layer, self.graph16, self.parity, self.graphs = layer, graph16, parity, graphs
        self.at = graph16 + layer * graphs * UNIT

    def has_before(self, n=1):
        return not isinstance(self.at, int) or self.at >= n * UNIT

    def first_of_layer(self):
        return isinstance(self.graph16, int) and self.graph16 == 0

    def is_first(self):
        return isinstance(self.at, int) and self.at == 0


def gnn_program(nc, x, adj, attn_w, attn_b, w1, b1, w2, b2, g1, beta1, g2, beta2, out):
    B, N, D = x.shape
    L, _, F = w1.shape
    NT = N // P
    DT = D // P
    FT = F // P
    NP = NT // 2
    assert NT == 4 and 2 * D == 512 and N == 512 and UNIT % FT == 0

    x_mid = nc.dram_tensor("x_mid", [(L - 1) * B * P, NT * D], F32)
    masks = nc.dram_tensor("masks", [B * P, NT * N], BF16)
    x_rows = x.rearrange("b n d -> (b n) d")
    out_rows = out.rearrange("b n d -> (b n) d")
    adj_rows = adj.rearrange("b i j -> (b i) j")

    def node_rows(flat, first):
        return flat[bass.ds(first, N), :].rearrange("(t p) d -> p t d", p=P)

    with ExitStack() as ctx:
        def sb(name, shape, dt=F32):
            return ctx.enter_context(nc.sbuf_tensor(name, shape, dt))

        def psum(name):
            return ctx.enter_context(nc.psum_tensor(name, [P, 512], F32))

        def sem(name):
            return ctx.enter_context(nc.semaphore(name))

        ident = sb("ident", [P, P])
        eye_int = sb("eye_int", [P, P], I32)
        eps_t = sb("eps_t", [P, NT])
        neg_half = sb("neg_half", [P, NT])
        neg_one = sb("neg_one", [P, NT])
        zero_col = sb("zero_col", [P, 1])
        gelu_probe = sb("gelu_probe", [P, 1])
        attn_w_bc = sb("attn_w_bc", [P, L, 2, D])
        attn_b_bc = sb("attn_b_bc", [P, L])
        g1_bc = sb("g1_bc", [P, L, D])
        beta1_bc = sb("beta1_bc", [P, L, D])
        b2_bc = sb("b2_bc", [P, L, D])
        g2_bc = sb("g2_bc", [P, L, D])
        beta2_bc = sb("beta2_bc", [P, L, D])
        b1_col = sb("b1_col", [P, L, FT])
        w_stage = sb("w_stage", [P, DT * F])
        w1_hi = sb("w1_hi", [P, DT, F], F32R)
        w1_lo = sb("w1_lo", [P, DT, F], F32R)
        w2_hi = sb("w2_hi", [P, FT, D], F32R)
        w2_lo = sb("w2_lo", [P, FT, D], F32R)
        adj_t = sb("adj_t", [P, NT, N], I32)
        no_edge = sb("no_edge", [P, NT, N], BF16)
        x_t = sb("x_t", [P, NT, D])
        x_hi = sb("x_hi", [P, NT, D], F32R)
        x_lo = sb("x_lo", [P, NT, D], F32R)
        dot_junk = sb("dot_junk", [P, 4, D], BF16)
        s_i = sb("s_i", [P, NT])
        s_j = sb("s_j", [P, NT])
        row_max = sb("row_max", [P, NT])
        top = sb("top", [P, NT])
        top_leaky = sb("top_leaky", [P, NT])
        shift_pos = sb("shift_pos", [P, NT])
        shift_neg = sb("shift_neg", [P, NT])
        score = sb("score", [P, NT, N])
        prob = sb("prob", [P, NT, N])
        denom = sb("denom", [P, NT])
        x_res = sb("x_res", [P, NT, D])
        recip = sb("recip", [P, NT])
        pt_hi = sb("pt_hi", [P, NT, N], F32R)
        pt_lo = sb("pt_lo", [P, NT, N], F32R)
        y1 = sb("y1", [P, NT, D])
        stats1 = sb("stats1", [P, NT, 6])
        mv1 = sb("mv1", [P, NT, 2])
        var1 = sb("var1", [P, NT])
        rstd1 = sb("rstd1", [P, NT])
        h = sb("h", [P, NT, D])
        ht_hi = sb("ht_hi", [P, DT, N], F32R)
        ht_lo = sb("ht_lo", [P, DT, N], F32R)
        h_b2 = sb("h_b2", [P, NT, D])
        hid = sb("hid", [P, G_RING, N])
        hid_hi = sb("hid_hi", [P, FT, N], F32R)
        hid_lo = sb("hid_lo", [P, FT, N], F32R)
        y2 = sb("y2", [P, NT, D])
        stats2 = sb("stats2", [P, NT, 6])
        mv2 = sb("mv2", [P, NT, 2])
        var2 = sb("var2", [P, NT])
        rstd2 = sb("rstd2", [P, NT])
        mr2 = sb("mr2", [P, NT])
        nmr2 = sb("nmr2", [P, NT])
        x_new = sb("x_new", [P, NT, D])
        stats3 = sb("stats3", [P, NT, 6])
        mv3 = sb("mv3", [P, NT, 2])
        var3 = sb("var3", [P, NT])
        rstd3 = sb("rstd3", [P, NT])
        mr3 = sb("mr3", [P, NT])
        nmr3 = sb("nmr3", [P, NT])

        ps_hid = [psum(f"ps_hid{i}") for i in range(F1_BANKS)]
        ps_turn = [psum(f"ps_turn{i}") for i in range(2)]
        ps_acc = [psum(f"ps_acc{i}") for i in range(NP)]
        ps_sj = psum("ps_sj")

        attn_in = [sem(f"attn_in{layer}") for layer in range(L)]
        b1_in = sem("b1_in")
        params_in = [sem(f"params_in{layer}") for layer in range(L)]
        consts_set = sem("consts_set")
        ident_set = sem("ident_set")
        w_in = [sem("w1_in"), sem("w2_in")]
        w_hi_set = sem("w_hi_set")
        w_lo_set = sem("w_lo_set")
        adj_in = sem("adj_in")
        x_in = sem("x_in")
        x_res_in = sem("x_res_in")
        x_first_in = sem("x_first_in")
        stored = sem("stored")
        diag_set = sem("diag_set")
        masked = sem("masked")
        mask_stored = sem("mask_stored")
        dotted = sem("dotted")
        spread = sem("spread")
        scored = sem("scored")
        shifted = sem("shifted")
        exped = sem("exped")
        prob_set = sem("prob_set")
        x_hi_set = sem("x_hi_set")
        x_lo_set = sem("x_lo_set")
        turned = sem("turned")
        pt_hi_set = sem("pt_hi_set")
        pt_lo_set = sem("pt_lo_set")
        recip_set = sem("recip_set")
        agg_done = sem("agg_done")
        y1_set = sem("y1_set")
        moments1 = sem("moments1")
        rstd1_set = sem("rstd1_set")
        centered1 = sem("centered1")
        h_set = sem("h_set")
        h_turned = sem("h_turned")
        ht_hi_set = sem("ht_hi_set")
        ht_lo_set = sem("ht_lo_set")
        h_b2_set = sem("h_b2_set")
        gelu_ready = sem("gelu_ready")
        hid_done = sem("hid_done")
        hid_set = sem("hid_set")
        hid_hi_set = sem("hid_hi_set")
        hid_lo_vec = sem("hid_lo_vec")
        hid_lo_pool = sem("hid_lo_pool")
        ff_done = sem("ff_done")
        y2_set = sem("y2_set")
        moments2 = sem("moments2")
        rstd2_set = sem("rstd2_set")
        normed2 = sem("normed2")
        scaled2 = sem("scaled2")
        x_new_set = sem("x_new_set")
        y3_set = sem("y3_set")
        moments3 = sem("moments3")
        rstd3_set = sem("rstd3_set")
        normed3 = sem("normed3")

        VEC_LO = [k for k in range(FT) if k not in POOL_LO]
        N_PARAMS = 5

        def staged(n):
            k = FT if n % 2 else DT
            flat = adj_t[:, :, :].bitcast(F32).rearrange("p t n -> p (t n)") if n % 2 and n > 1 else w_stage[:, :]
            return flat.rearrange("p (k f) -> p k f", k=k)

        def x_first(u):
            both = adj_t[:, :, :].bitcast(F32).rearrange("p (s h) (g d) -> p s (h g) d", s=2, d=D)
            return both[:, u.parity]

        def last(u):
            return u.layer == L - 1

        def at_last(u):
            return u.graph16

        def slots(eng, slot):
            def unit(i):
                return Unit(i // B, i % B * UNIT, i % 2, B) if 0 <= i < L * B else None

            def peeled(i):
                slot(unit(i - 2), unit(i - 1), unit(i), unit(i + 1), unit(i + 2))

            peeled(-2)
            peeled(-1)
            for layer in range(L):
                peeled(layer * B)
                peeled(layer * B + 1)
                assert B % 2 == 0
                with eng.Fori(1, B // 2 - 1) as half:
                    for odd in (0, 1):
                        slot(*(Unit(layer, (2 * half + odd + k) * UNIT, (odd + k) % 2, B)
                               for k in (-2, -1, 0, 1, 2)))
                peeled(layer * B + B - 2)
                peeled(layer * B + B - 1)
            peeled(L * B)
            peeled(L * B + 1)

        block = ctx.enter_context(nc.Block())

        @block.sync
        def _(sp):
            def load_weights(n):
                if n == 3:
                    sp.wait_ge(masked, B * UNIT)
                elif n:
                    before = n - 1 if n < 3 else n - 2
                    sp.wait_ge(w_hi_set, before + 1)
                    sp.wait_ge(w_lo_set, before + 1)
                layer, second = divmod(n, 2)
                sp.dma_start(staged(n), (w2 if second else w1)[layer].rearrange("(k p) f -> p k f", p=P))\
                    .then_inc(w_in[second], 16)

            def known(value):
                return value if isinstance(value, int) else sp.snap(sp.to_reg(value))

            def source_of_x(u):
                if u.layer == 0:
                    return node_rows(x_rows, known(u.graph16 * (N // UNIT))), None
                here = known(u.graph16 * (P // UNIT) + (u.layer - 1) * B * P)
                return x_mid[bass.ds(here, P), :], known(u.at + UNIT - B * UNIT)

            def load_x(tile, source, layer_before, signal):
                if layer_before is not None:
                    sp.wait_ge(stored, layer_before)
                    sp.dma_start(tile[:, :, :].rearrange("p t d -> p (t d)"), source).then_inc(signal, 16)
                else:
                    sp.dma_start(tile[:, :, :], source).then_inc(signal, 16)

            def load_prepare(u):
                source, layer_before = source_of_x(u)
                at = known(u.at)
                if u.layer == 0:
                    adj_source = node_rows(adj_rows, known(u.graph16 * (N // UNIT)))
                    if u.is_first():
                        load_x(x_t, source, layer_before, x_in)
                    if u.has_before():
                        sp.wait_ge(masked, at)
                    sp.dma_start(adj_t[:, :, :], adj_source).then_inc(adj_in, 16)
                else:
                    mask_source = masks[bass.ds(known(u.graph16 * (P // UNIT)), P), :]
                    if u.layer == 1 and u.first_of_layer():
                        sp.wait_ge(mask_stored, B * UNIT)
                    sp.wait_ge(scored, at)
                    sp.dma_start(no_edge[:, :, :].rearrange("p t n -> p (t n)"), mask_source)\
                        .then_inc(masked, 16)
                if u.has_before():
                    sp.wait_ge(dotted, at)
                    sp.wait_ge(x_lo_set, at)
                    load_x(x_t, source, layer_before, x_in)

            def store_mask(u):
                at, full = known(u.at), known(u.at + UNIT)
                target = masks[bass.ds(known(u.graph16 * (P // UNIT)), P), :]
                if u.has_before():
                    sp.wait_ge(mask_stored, at)
                sp.wait_ge(masked, full)
                sp.dma_start(target, no_edge[:, :, :].rearrange("p t n -> p (t n)")).then_inc(mask_stored, 16)

            def load_residual(u):
                source, layer_before = source_of_x(u)
                at = known(u.at)
                if u.has_before():
                    sp.wait_ge(y1_set, at)
                load_x(x_res, source, layer_before, x_res_in)

            def load_first(u):
                source = node_rows(x_rows, known(u.graph16 * (N // UNIT)))
                two_before = known(u.at - UNIT)
                if u.first_of_layer():
                    sp.wait_ge(w_lo_set, 2 * L)
                else:
                    sp.wait_ge(stored, two_before)
                sp.dma_start(x_first(u), source).then_inc(x_first_in, 16)

            def store(u):
                at = known(u.at)
                if last(u):
                    ready, full, tile = normed3, known(at_last(u) + UNIT), x_first(u)
                    target = node_rows(out_rows, known(u.graph16 * (N // UNIT)))
                else:
                    ready, full = x_new_set, known(u.at + UNIT)
                    tile = x_new[:, :, :].rearrange("p t d -> p (t d)")
                    target = x_mid[bass.ds(known(u.graph16 * (P // UNIT) + u.layer * B * P), P), :]
                if u.has_before():
                    sp.wait_ge(stored, at)
                sp.wait_ge(ready, full)
                sp.dma_start(target, tile).then_inc(stored, 16)

            def load_attn(layer):
                sp.dma_start(attn_w_bc[:, layer, :, :].rearrange("p s d -> p (s d)"),
                             attn_w[layer].partition_broadcast(P)).then_inc(attn_in[layer], 16)

            def load_params(layer):
                for tile, param in ((g1_bc, g1), (beta1_bc, beta1), (b2_bc, b2), (g2_bc, g2), (beta2_bc, beta2)):
                    sp.dma_start(tile[:, layer, :], param[layer].partition_broadcast(P))\
                        .then_inc(params_in[layer], 16)

            load_attn(0)
            sp.dma_start(attn_b_bc[:, :], attn_b.partition_broadcast(P)).then_inc(attn_in[0], 16)
            load_prepare(Unit(0, 0, 0, B))
            load_weights(0)
            load_params(0)
            with nc.allow_non_contiguous_dma(reason="b1 by partition, once"):
                sp.dma_start(b1_col[:, :, :], b1.rearrange("l (k p) -> p l k", p=P)).then_inc(b1_in, 16)

            def slot(old, prev, u, v, w):
                if v and v.first_of_layer() and v.layer > 0:
                    load_weights(2 * v.layer + 1)
                if w and not w.is_first():
                    load_prepare(w)
                if v:
                    load_residual(v)
                if v and v.is_first():
                    load_weights(1)
                if u and u.is_first():
                    for layer in range(1, L):
                        load_attn(layer)
                        load_params(layer)
                if w and w.layer == 0:
                    store_mask(w)
                if prev and last(prev):
                    load_first(prev)
                if old and last(old):
                    store(old)
                if prev and not last(prev):
                    store(prev)
                if u and u.first_of_layer() and u.layer + 1 < L:
                    load_weights(2 * u.layer + 2)

            slots(sp, slot)
            sp.wait_ge(stored, L * B * UNIT)

        @block.gpsimd
        def _(pool):
            tt = nc.gpsimd.tensor_tensor

            def weight_lo(n):
                hi, lo = (w2_hi, w2_lo) if n % 2 else (w1_hi, w1_lo)
                pool.wait_ge(w_hi_set, n + 1)
                tt(lo[:, :, :], staged(n), hi[:, :, :], ALU.subtract).then_inc(w_lo_set, 1)

            def self_loops(u):
                for t in range(NT):
                    if t == 0:
                        pool.wait_ge(adj_in, u.at + UNIT)
                    blk = adj_t[:, t, t * P:(t + 1) * P]
                    tt(blk, blk, eye_int[:, :], ALU.add).then_inc(diag_set, steps(1, NT))

            def split_x(u):
                pool.wait_ge(x_hi_set, u.at + UNIT)
                tt(x_lo[:, :, :], x_t[:, :, :], x_hi[:, :, :], ALU.subtract).then_inc(x_lo_set, UNIT)

            def rstd_of(u_at, pair, moments, mv, var, rstd, signal, of):
                s = slice(2 * pair, 2 * pair + 2)
                pool.wait_ge(moments, u_at + steps(4 * pair + 4, 8))
                tt(var[:, s], mv[:, s, 1], eps_t[:, s], ALU.add).then_inc(signal, steps(1, of))
                pool.wait_ge(signal, u_at + steps((pair * of) // 2 + 1, of))
                tt(rstd[:, s], var[:, s], neg_half[:, s], ALU.pow).then_inc(signal, steps(1, of))

            def offset_of(u_at, pair, mv, rstd, mr, nmr, signal):
                s = slice(2 * pair, 2 * pair + 2)
                pool.wait_ge(signal, u_at + steps(4 * pair + 2, 8))
                tt(mr[:, s], mv[:, s, 0], rstd[:, s], ALU.mult).then_inc(signal, steps(1, 8))
                pool.wait_ge(signal, u_at + steps(4 * pair + 3, 8))
                tt(nmr[:, s], mr[:, s], neg_one[:, s], ALU.mult).then_inc(signal, steps(1, 8))

            def scale2(u, pair):
                rstd_of(u.at, pair, moments2, mv2, var2, rstd2, rstd2_set, 8)
                offset_of(u.at, pair, mv2, rstd2, mr2, nmr2, rstd2_set)

            def scale3(u, pair):
                rstd_of(at_last(u), pair, moments3, mv3, var3, rstd3, rstd3_set, 8)
                offset_of(at_last(u), pair, mv3, rstd3, mr3, nmr3, rstd3_set)

            def add_b2(u):
                if u.first_of_layer():
                    pool.wait_ge(params_in[u.layer], 16 * N_PARAMS)
                if u.has_before():
                    pool.wait_ge(y2_set, u.at)
                for t in range(NT):
                    pool.wait_ge(h_set, u.at + steps(t + 1, NT))
                    tt(h_b2[:, t, :], h[:, t, :], b2_bc[:, u.layer, :], ALU.add).then_inc(h_b2_set, steps(1, NT))

            def affine2(u, pair):
                for t in (2 * pair, 2 * pair + 1):
                    pool.wait_ge(normed2, u.at + steps(t + 1, NT))
                    tt(x_new[:, t, :], x_new[:, t, :], g2_bc[:, u.layer, :], ALU.mult)\
                        .then_inc(scaled2, steps(1, NT))
                for t in (2 * pair, 2 * pair + 1):
                    pool.wait_ge(scaled2, u.at + steps(t + 1, NT))
                    tt(x_new[:, t, :], x_new[:, t, :], beta2_bc[:, u.layer, :], ALU.add)\
                        .then_inc(x_new_set, steps(1, NT))

            def residual3(u, pair):
                if pair == 0:
                    pool.wait_ge(x_first_in, at_last(u) + UNIT)
                for t in (2 * pair, 2 * pair + 1):
                    pool.wait_ge(x_new_set, u.at + steps(t + 1, NT))
                    tt(x_first(u)[:, t, :], x_new[:, t, :], x_first(u)[:, t, :], ALU.add)\
                        .then_inc(y3_set, steps(1, NT))

            def hidden_lo(u, n):
                k = POOL_LO[n]
                if n == 0 and u.has_before():
                    pool.wait_ge(ff_done, u.at)
                pool.wait_ge(hid_hi_set, u.at + steps(k + 1, FT))
                tt(hid_lo[:, k, :], hid[:, k % G_RING, :], hid_hi[:, k, :], ALU.subtract)\
                    .then_inc(hid_lo_pool, steps(1, len(POOL_LO)))

            nc.gpsimd.memset(ident[:, :], 0.0).then_inc(ident_set, 1)
            nc.gpsimd.memset(eye_int[:, :], 0).then_inc(ident_set, 1)
            nc.gpsimd.memset(eps_t[:, :], EPS).then_inc(consts_set, 1)
            nc.gpsimd.memset(neg_half[:, :], -0.5).then_inc(consts_set, 1)
            nc.gpsimd.memset(neg_one[:, :], -1.0).then_inc(consts_set, 1)
            nc.gpsimd.memset(zero_col[:, :], 0.0).then_inc(consts_set, 1)
            pool.wait_ge(ident_set, 2)
            nc.gpsimd.affine_select(out=ident[:, :], in_=ident[:, :], compare_op=ALU.not_equal, fill=1.0,
                                    base=0, pattern=[[-1, P]], channel_multiplier=1).then_inc(ident_set, 1)
            pool.wait_ge(ident_set, 3)
            nc.gpsimd.tensor_copy(eye_int[:, :], ident[:, :]).then_inc(ident_set, 1)
            pool.wait_ge(ident_set, 4)
            pool.wait_ge(consts_set, 4)

            def slot(old, prev, u, v, w):
                if not u and not w:
                    if old:
                        scale3(old, 0)
                        scale3(old, 1)
                    if prev:
                        for pair in range(NP):
                            scale2(prev, pair)
                            affine2(prev, pair)
                            residual3(prev, pair)
                    return
                if old and last(old):
                    scale3(old, 0)
                if u and u.first_of_layer() and u.layer > 0:
                    weight_lo(2 * u.layer + 1)
                if w and w.layer == 0:
                    self_loops(w)
                if v and v.is_first():
                    weight_lo(0)
                if prev:
                    scale2(prev, 0)
                    scale2(prev, 1)
                if u:
                    hidden_lo(u, 0)
                if u:
                    add_b2(u)
                if old and last(old):
                    scale3(old, 1)
                if u:
                    hidden_lo(u, 1)
                if v:
                    rstd_of(v.at, 0, moments1, mv1, var1, rstd1, rstd1_set, 4)
                if prev:
                    affine2(prev, 0)
                if v:
                    rstd_of(v.at, 1, moments1, mv1, var1, rstd1, rstd1_set, 4)
                if v and v.first_of_layer() and v.layer > 0:
                    weight_lo(2 * v.layer)
                if prev and last(prev):
                    residual3(prev, 0)
                if prev:
                    affine2(prev, 1)
                if prev and last(prev):
                    residual3(prev, 1)
                if w:
                    split_x(w)
                if v and v.is_first():
                    weight_lo(1)

            slots(pool, slot)

        @block.scalar
        def _(act):
            def weight_hi(n):
                hi = w2_hi if n % 2 else w1_hi
                act.wait_ge(w_in[n % 2], 16 * (n // 2 + 1))
                if n > 1:
                    act.wait_ge(ff_done if n % 2 else hid_done, n // 2 * B * UNIT)
                nc.scalar.activation(hi[:, :, :], staged(n), ACT.Copy).then_inc(w_hi_set, 1)

            def mask(u):
                act.wait_ge(diag_set, u.at + UNIT)
                if u.has_before():
                    act.wait_ge(scored, u.at)
                    act.wait_ge(mask_stored, u.at)
                nc.scalar.activation(no_edge[:, :, :], adj_t[:, :, :], ACT.Relu, bias=BIG, scale=-BIG)\
                    .then_inc(masked, UNIT)

            def exps(u, pair):
                if pair == 0:
                    act.wait_ge(shifted, u.at + UNIT)
                    if u.has_before():
                        act.wait_ge(turned, u.at)
                for t in (2 * pair, 2 * pair + 1):
                    nc.scalar.activation(prob[:, t, :], score[:, t, :], ACT.Exp, bias=shift_pos[:, t:t + 1])\
                        .then_inc(exped, steps(1, 2 * NT))
                for t in (2 * pair, 2 * pair + 1):
                    act.wait_ge(exped, u.at + steps(2 * pair + t + 1, 2 * NT))
                    nc.scalar.activation(score[:, t, :], score[:, t, :], ACT.Exp, bias=shift_neg[:, t:t + 1],
                                         scale=SLOPE).then_inc(exped, steps(1, 2 * NT))

            def split_x(u):
                act.wait_ge(x_in, u.at + UNIT)
                if u.has_before():
                    act.wait_ge(agg_done, u.at)
                nc.scalar.activation(x_hi[:, :, :], x_t[:, :, :], ACT.Copy).then_inc(x_hi_set, UNIT)

            def prob_hi(u, jt):
                if jt == 0 and u.has_before():
                    act.wait_ge(agg_done, u.at)
                act.wait_ge(turned, u.at + steps(jt + 1, NT))
                nc.scalar.activation(pt_hi[:, jt, :], ps_turn[jt % 2][:, :], ACT.Copy)\
                    .then_inc(pt_hi_set, steps(1, NT))

            def h_hi(u, pair):
                if pair == 0 and u.has_before():
                    act.wait_ge(hid_done, u.at)
                act.wait_ge(h_turned, u.at + steps(pair + 1, NP))
                nc.scalar.activation(ht_hi[:, :, pair * 2 * P:(pair + 1) * 2 * P],
                                     ps_turn[pair][:, :].rearrange("p (k n) -> p k n", k=DT), ACT.Copy)\
                    .then_inc(ht_hi_set, steps(1, NP))

            def gelu(u, k):
                if k >= G_RING or u.has_before():
                    free = k - G_RING
                    back = u.at if free >= 0 else u.at - UNIT
                    free %= FT
                    if free in POOL_LO:
                        act.wait_ge(hid_lo_pool, back + steps(POOL_LO.index(free) + 1, len(POOL_LO)))
                    else:
                        act.wait_ge(hid_lo_vec, back + steps(free + 1, FT))
                act.wait_ge(hid_done, u.at + steps(k + 1, FT))
                if k == 0 and u.is_first():
                    act.wait_ge(b1_in, 16)
                nc.scalar.activation(hid[:, k % G_RING, :], ps_hid[k % F1_BANKS][:, :], ACT.Gelu,
                                     bias=b1_col[:, u.layer, k:k + 1]).then_inc(hid_set, steps(1, FT))

            def hidden_hi(u, k):
                if k == 0 and u.has_before():
                    act.wait_ge(ff_done, u.at)
                act.wait_ge(hid_set, u.at + steps(k + 1, FT))
                nc.scalar.activation(hid_hi[:, k, :], hid[:, k % G_RING, :], ACT.Copy)\
                    .then_inc(hid_hi_set, steps(1, FT))

            def normalize2(u, pair):
                act.wait_ge(rstd2_set, u.at + steps(4 * pair + 4, 8))
                if pair == 0 and last(u) and not u.first_of_layer():
                    act.wait_ge(y3_set, at_last(u))
                elif pair == 0 and u.has_before():
                    act.wait_ge(stored, u.at)
                for t in (2 * pair, 2 * pair + 1):
                    nc.scalar.activation(x_new[:, t, :], y2[:, t, :], ACT.Identity, bias=nmr2[:, t:t + 1],
                                         scale=rstd2[:, t:t + 1]).then_inc(normed2, steps(1, NT))

            def normalize3(u, pair):
                act.wait_ge(rstd3_set, at_last(u) + steps(4 * pair + 4, 8))
                for t in (2 * pair, 2 * pair + 1):
                    nc.scalar.activation(x_first(u)[:, t, :], x_first(u)[:, t, :], ACT.Identity, bias=nmr3[:, t:t + 1],
                                         scale=rstd3[:, t:t + 1]).then_inc(normed3, steps(1, NT))

            def load_gelu_table(u):
                if u.has_before():
                    act.wait_ge(gelu_ready, u.at)
                nc.scalar.activation(gelu_probe[:, :], zero_col[:, :], ACT.Gelu).then_inc(gelu_ready, UNIT)

            act.wait_ge(consts_set, 4)

            def slot(old, prev, u, v, w):
                if old and last(old) and not u:
                    normalize3(old, 0)
                    normalize3(old, 1)
                if u and u.first_of_layer() and u.layer > 0:
                    weight_hi(2 * u.layer + 1)
                if v:
                    prob_hi(v, 0)
                    prob_hi(v, 1)
                for k in range(FT):
                    if u:
                        gelu(u, k)
                    if v and k == 0:
                        prob_hi(v, 2)
                        prob_hi(v, 3)
                    if u and k > 0:
                        hidden_hi(u, k - 1)
                    if w and w.layer == 0 and k == 2:
                        mask(w)
                    if prev and k in (3, 4):
                        normalize2(prev, k - 3)
                    if u and old and last(old) and k in (2, 6):
                        normalize3(old, k // 4)
                if u:
                    hidden_hi(u, FT - 1)
                if v and v.is_first():
                    weight_hi(1)
                elif v and v.first_of_layer():
                    weight_hi(2 * v.layer)
                if w:
                    split_x(w)
                    for pair in range(NP):
                        exps(w, pair)
                if w and w.is_first():
                    weight_hi(0)
                if v:
                    h_hi(v, 0)
                    h_hi(v, 1)
                    load_gelu_table(v)

            slots(act, slot)

        @block.tensor
        def _(pe):
            def hidden(u, k):
                if k == 0:
                    pe.wait_ge(ht_lo_set, u.at + UNIT)
                    if u.first_of_layer():
                        pe.wait_ge(w_lo_set, 2 * u.layer + 1)
                if k >= F1_BANKS or u.has_before():
                    free = k - F1_BANKS
                    if free < 0:
                        free = max(j for j in range(FT) if j % F1_BANKS == k) - FT
                    pe.wait_ge(hid_set, u.at + steps(free + 1, FT))
                cols = slice(k * P, (k + 1) * P)
                terms = [(w, ht, d) for d in range(DT) for w, ht in ((w1_hi, ht_hi), (w1_hi, ht_lo), (w1_lo, ht_hi))]
                for n, (w, ht, d) in enumerate(terms):
                    mm = nc.tensor.matmul(ps_hid[k % F1_BANKS][:, :], w[:, d, cols], ht[:, d, :],
                                          start=(n == 0), stop=(n == len(terms) - 1))
                mm.then_inc(hid_done, steps(1, FT))

            def turn_prob(u, jt):
                if jt == 0:
                    pe.wait_ge(prob_set, u.at + UNIT)
                if jt >= 2:
                    pe.wait_ge(pt_lo_set, u.at + steps(jt - 1, NT))
                elif u.has_before():
                    pe.wait_ge(ht_lo_set, u.at - UNIT + steps(jt + 1, NP))
                for it in range(NT):
                    mm = nc.tensor.transpose(ps_turn[jt % 2][:, it * P:(it + 1) * P],
                                             prob[:, it, jt * P:(jt + 1) * P], ident[:, :])
                mm.then_inc(turned, steps(1, NT))

            def spread_sj(u):
                pe.wait_ge(dotted, u.at + UNIT)
                if u.has_before():
                    pe.wait_ge(scored, u.at)
                for t in range(NT):
                    mm = nc.tensor.transpose(ps_sj[:, t * P:(t + 1) * P], s_j[:, t:t + 1].to_broadcast([P, P]),
                                             ident[:, :])
                mm.then_inc(spread, UNIT)

            def aggregate(u, t):
                pair, half = divmod(t, 2)
                if t == 0:
                    pe.wait_ge(pt_lo_set, u.at + UNIT)
                    pe.wait_ge(x_lo_set, u.at + UNIT)
                if half == 0 and u.has_before(2):
                    pe.wait_ge(y2_set, u.at - 2 * UNIT + steps(2 * pair + 2, NT))
                cols = slice(t * P, (t + 1) * P)
                terms = [(p, xs, jt) for jt in range(NT)
                         for p, xs in ((pt_hi, x_hi), (pt_hi, x_lo), (pt_lo, x_hi))]
                for n, (p, xs, jt) in enumerate(terms):
                    mm = nc.tensor.matmul(ps_acc[pair][:, half * D:(half + 1) * D], p[:, jt, cols],
                                          xs[:, jt, :], start=(n == 0), stop=(n == len(terms) - 1))
                if half:
                    mm.then_inc(agg_done, steps(1, NP))

            def feed(u, t, next_unit):
                pair, half = divmod(t, 2)
                if t == 0 and u.first_of_layer():
                    pe.wait_ge(w_lo_set, 2 * u.layer + 2)
                if half == 0 and next_unit:
                    pe.wait_ge(y1_set, next_unit.at + steps(2 * pair + 2, NT))
                cols = slice(t * P, (t + 1) * P)
                terms = [(g, w, k) for k in VEC_LO + list(POOL_LO)
                         for g, w in ((hid_hi, w2_hi), (hid_hi, w2_lo), (hid_lo, w2_hi))]
                for n, (g, w, k) in enumerate(terms):
                    if t == 0 and n % 3 == 0:
                        if k in POOL_LO:
                            pe.wait_ge(hid_lo_pool, u.at + steps(POOL_LO.index(k) + 1, len(POOL_LO)))
                        else:
                            pe.wait_ge(hid_lo_vec, u.at + steps(k + 1, FT))
                    mm = nc.tensor.matmul(ps_acc[pair][:, half * D:(half + 1) * D], g[:, k, cols], w[:, k, :],
                                          start=(n == 0), stop=(n == len(terms) - 1))
                if half:
                    mm.then_inc(ff_done, steps(1, NP))

            def turn_h(u, pair):
                pe.wait_ge(h_set, u.at + steps(2 * pair + 2, NT))
                pe.wait_ge(pt_lo_set, u.at + steps(pair + 3, NT))
                for d in range(DT):
                    for half in range(2):
                        mm = nc.tensor.transpose(ps_turn[pair][:, (2 * d + half) * P:(2 * d + half + 1) * P],
                                                 h[:, 2 * pair + half, d * P:(d + 1) * P], ident[:, :])
                mm.then_inc(h_turned, steps(1, NP))

            pe.wait_ge(ident_set, 3)

            def slot(old, prev, u, v, w):
                if v:
                    turn_prob(v, 0)
                    turn_prob(v, 1)
                for k in range(FT):
                    if u:
                        hidden(u, k)
                    if v and k == 0:
                        turn_prob(v, 2)
                        turn_prob(v, 3)
                    for t in range(NT):
                        if v and AGG_AFTER[t] == k:
                            aggregate(v, t)
                    if w and k == 5:
                        spread_sj(w)
                if u:
                    feed(u, 0, v)
                    feed(u, 1, v)
                    feed(u, 2, v)
                if v:
                    turn_h(v, 0)
                    turn_h(v, 1)
                if u:
                    feed(u, 3, v)

            slots(pe, slot)

        @block.vector
        def _(dve):
            v_ = nc.vector

            def dots(u, t):
                if t == 0:
                    if u.first_of_layer():
                        dve.wait_ge(attn_in[u.layer], 16 if u.layer else 32)
                    dve.wait_ge(x_in, u.at + UNIT)
                    if u.has_before():
                        dve.wait_ge(spread, u.at)
                        dve.wait_ge(prob_set, u.at)
                elif t >= 2:
                    dve.wait_ge(dotted, u.at + steps(2 * t - 2, 2 * NT))
                v_.tensor_tensor_reduce(dot_junk[:, 2 * t % 4, :], x_t[:, t, :], attn_w_bc[:, u.layer, 0, :],
                                        1.0, attn_b_bc[:, u.layer:u.layer + 1], ALU.mult, ALU.add,
                                        s_i[:, t:t + 1]).then_inc(dotted, steps(1, 2 * NT))
                v_.tensor_tensor_reduce(dot_junk[:, (2 * t + 1) % 4, :], x_t[:, t, :], attn_w_bc[:, u.layer, 1, :],
                                        1.0, 0.0, ALU.mult, ALU.add,
                                        s_j[:, t:t + 1]).then_inc(dotted, steps(1, 2 * NT))

            def scores(u, t):
                if t == 0:
                    dve.wait_ge(spread, u.at + UNIT)
                    dve.wait_ge(masked, u.at + UNIT)
                v_.tensor_tensor_reduce(score[:, t, :], ps_sj[:, :], no_edge[:, t, :], 1.0, LOWEST,
                                        ALU.subtract, ALU.max, row_max[:, t:t + 1])\
                    .then_inc(scored, steps(1, NT))

            def shifts(u):
                dve.wait_ge(scored, u.at + UNIT)
                v_.tensor_tensor(top[:, :], row_max[:, :], s_i[:, :], ALU.add).then_inc(shifted, steps(1, 4))
                dve.wait_ge(shifted, u.at + steps(1, 4))
                v_.scalar_tensor_tensor(out=top_leaky[:, :], in0=top[:, :], scalar=SLOPE, in1=top[:, :],
                                        op0=ALU.mult, op1=ALU.max).then_inc(shifted, steps(1, 4))
                dve.wait_ge(shifted, u.at + steps(2, 4))
                v_.tensor_tensor(shift_pos[:, :], s_i[:, :], top_leaky[:, :], ALU.subtract)\
                    .then_inc(shifted, steps(1, 4))
                v_.scalar_tensor_tensor(out=shift_neg[:, :], in0=s_i[:, :], scalar=SLOPE, in1=top_leaky[:, :],
                                        op0=ALU.mult, op1=ALU.subtract).then_inc(shifted, steps(1, 4))

            def probs(u, t):
                dve.wait_ge(exped, u.at + steps(t + 3 + 2 * (t // 2), 2 * NT))
                v_.scalar_tensor_tensor(out=prob[:, t, :], in0=prob[:, t, :], scalar=1.0, in1=score[:, t, :],
                                        op0=ALU.mult, op1=ALU.max, accum_out=denom[:, t:t + 1])\
                    .then_inc(prob_set, steps(1, NT))

            def prob_lo(u, jt):
                if jt == 0 and u.has_before():
                    dve.wait_ge(agg_done, u.at)
                dve.wait_ge(pt_hi_set, u.at + steps(jt + 1, NT))
                v_.tensor_tensor(pt_lo[:, jt, :], ps_turn[jt % 2][:, :], pt_hi[:, jt, :], ALU.subtract)\
                    .then_inc(pt_lo_set, steps(1, NT))

            def reciprocals(u):
                dve.wait_ge(prob_set, u.at + UNIT)
                v_.reciprocal(recip[:, :], denom[:, :]).then_inc(recip_set, UNIT)

            def residual1(u, pair):
                dve.wait_ge(agg_done, u.at + steps(pair + 1, NP))
                if pair == 0:
                    dve.wait_ge(recip_set, u.at + UNIT)
                    dve.wait_ge(x_res_in, u.at + UNIT)
                for half in range(2):
                    t = 2 * pair + half
                    v_.scalar_tensor_tensor(out=y1[:, t, :], in0=ps_acc[pair][:, half * D:(half + 1) * D],
                                            scalar=recip[:, t:t + 1], in1=x_res[:, t, :],
                                            op0=ALU.mult, op1=ALU.add).then_inc(y1_set, steps(1, NT))

            def moments(at, pair, ready, y, stats, mv, signal):
                for half in range(2):
                    t = 2 * pair + half
                    dve.wait_ge(ready, at + steps(t + 1, NT))
                    v_.bn_stats(stats[:, t, :], y[:, t, :]).then_inc(signal, steps(1, 8))
                for half in range(2):
                    t = 2 * pair + half
                    dve.wait_ge(signal, at + steps(4 * pair + 1 + half, 8))
                    v_.bn_aggr(mv[:, t, :], stats[:, t, :]).then_inc(signal, steps(1, 8))

            def affine1(u, pair):
                if pair == 0 and u.first_of_layer():
                    dve.wait_ge(params_in[u.layer], 16 * N_PARAMS)
                dve.wait_ge(rstd1_set, u.at + steps(2 * pair + 2, 4))
                if pair == 0 and u.has_before():
                    dve.wait_ge(h_turned, u.at)
                    dve.wait_ge(h_b2_set, u.at)
                for t in (2 * pair, 2 * pair + 1):
                    v_.scalar_tensor_tensor(out=h[:, t, :], in0=y1[:, t, :], scalar=mv1[:, t, 0:1],
                                            in1=g1_bc[:, u.layer, :], op0=ALU.subtract, op1=ALU.mult)\
                        .then_inc(centered1, steps(1, NT))
                for t in (2 * pair, 2 * pair + 1):
                    dve.wait_ge(centered1, u.at + steps(t + 1, NT))
                    v_.scalar_tensor_tensor(out=h[:, t, :], in0=h[:, t, :], scalar=rstd1[:, t:t + 1],
                                            in1=beta1_bc[:, u.layer, :], op0=ALU.mult, op1=ALU.add)\
                        .then_inc(h_set, steps(1, NT))

            def h_lo(u, pair):
                dve.wait_ge(ht_hi_set, u.at + steps(pair + 1, NP))
                cols = slice(pair * 2 * P, (pair + 1) * 2 * P)
                v_.tensor_tensor(ht_lo[:, :, cols], ps_turn[pair][:, :].rearrange("p (k n) -> p k n", k=DT),
                                 ht_hi[:, :, cols], ALU.subtract).then_inc(ht_lo_set, steps(1, NP))

            def hidden_lo(u, k):
                if k == 0 and u.has_before():
                    dve.wait_ge(ff_done, u.at)
                dve.wait_ge(hid_hi_set, u.at + steps(k + 1, FT))
                following = min([j for j in VEC_LO if j > k] + [FT])
                v_.tensor_tensor(hid_lo[:, k, :], hid[:, k % G_RING, :], hid_hi[:, k, :], ALU.subtract)\
                    .then_inc(hid_lo_vec, steps(following - k, FT))

            def residual2(u, pair):
                dve.wait_ge(ff_done, u.at + steps(pair + 1, NP))
                dve.wait_ge(h_b2_set, u.at + steps(2 * pair + 2, NT))
                if pair == 0 and u.has_before():
                    dve.wait_ge(normed2, u.at)
                for half in range(2):
                    t = 2 * pair + half
                    v_.tensor_tensor(y2[:, t, :], ps_acc[pair][:, half * D:(half + 1) * D], h_b2[:, t, :],
                                     ALU.add).then_inc(y2_set, steps(1, NT))

            def slot(old, prev, u, v, w):
                if old and last(old) and not u:
                    moments(at_last(old), 1, y3_set, x_first(old), stats3, mv3, moments3)
                if v:
                    prob_lo(v, 0)
                    prob_lo(v, 1)
                if prev:
                    residual2(prev, 0)
                    moments(prev.at, 0, y2_set, y2, stats2, mv2, moments2)
                if v:
                    prob_lo(v, 2)
                    prob_lo(v, 3)
                for k in range(FT):
                    if u and k in VEC_LO:
                        hidden_lo(u, k)
                    if prev and k == 0:
                        residual2(prev, 1)
                        moments(prev.at, 1, y2_set, y2, stats2, mv2, moments2)
                    if w and k in (1, 2):
                        dots(w, 2 * k - 2)
                        dots(w, 2 * k - 1)
                    if u and old and last(old) and k == 2:
                        moments(at_last(old), 1, y3_set, x_first(old), stats3, mv3, moments3)
                    if v and k == 3:
                        reciprocals(v)
                        residual1(v, 0)
                        moments(v.at, 0, y1_set, y1, stats1, mv1, moments1)
                    if w and k >= FT - NT:
                        scores(w, k - (FT - NT))
                if w:
                    shifts(w)
                if v:
                    residual1(v, 1)
                    moments(v.at, 1, y1_set, y1, stats1, mv1, moments1)
                if v:
                    affine1(v, 0)
                    affine1(v, 1)
                if w:
                    for t in range(NT):
                        probs(w, t)
                if v:
                    h_lo(v, 0)
                    h_lo(v, 1)
                if prev and last(prev):
                    moments(at_last(prev), 0, y3_set, x_first(prev), stats3, mv3, moments3)

            slots(dve, slot)


_INS = ["x", "adj", "L0_gnn_attn_w", "L0_gnn_attn_b", "L0_gnn_W1", "L0_gnn_b1", "L0_gnn_W2", "L0_gnn_b2",
        "L0_gnn_g1", "L0_gnn_beta1", "L0_gnn_g2", "L0_gnn_beta2"]


def kernel(**inputs):
    import numpy as _np
    import concourse.bacc as _bacc
    from concourse import mybir as _mybir
    from concourse.bass_utils import run_bass_kernel_spmd as _run

    nc = _bacc.Bacc("TRN2", target_bir_lowering=False, num_devices=1)
    arrays, args = {}, []
    for name in _INS:
        a = _np.ascontiguousarray(inputs[name])
        arrays[f"in_{name}"] = a
        args.append(nc.dram_tensor(f"in_{name}", a.shape, _mybir.dt.from_np(a.dtype), kind="ExternalInput").ap())
    out = nc.dram_tensor("out", inputs["x"].shape, _mybir.dt.float32, kind="ExternalOutput").ap()
    gnn_program(nc, *args, out)
    r = _run(nc, [arrays], core_ids=[0])
    return r.results[0]["out"]
```
